# Optimizing a Trainium2 kernel written in Bass

```python
import numpy as np
import jax
import jax.numpy as jnp

def _softmax(x, axis=-1):
    return jax.nn.softmax(x, axis=axis)

def _gelu(x):
    return jax.nn.gelu(x, approximate=True)

def _silu(x):
    return jax.nn.silu(x)

def _sigmoid(x):
    return jax.nn.sigmoid(x)

def _layernorm(x, axis=-1, eps=1e-05):
    m = jnp.mean(x, axis=axis, keepdims=True)
    v = jnp.var(x, axis=axis, keepdims=True)
    return (x - m) / jnp.sqrt(v + eps)

def _scatter_add(tgt, idx, src, axis=0):
    return tgt.at[idx].add(src)

def _segment_sum(src, seg, n):
    return jax.ops.segment_sum(src, seg, n)
kernel_name = 'mk_decoder_preln_d1_seqx_r8_6b8875'

def setup_inputs(seed: int=0):
    np.random.seed(seed)
    _w = jnp.asarray

    def _rec_inputs():
        import jax
        import jax.numpy as jnp
        _rk = jax.random.key(seed)
        x = -0.0002928 + 1 * jax.random.normal(jax.random.fold_in(_rk, 1), (8, 256, 128), jnp.float32)
        _lenS = 256 - jax.random.randint(jax.random.fold_in(_rk, 7), (8,), 0, max(1, 256 // 4) + 1, jnp.int32)
        _lenS2 = 256 - jax.random.randint(jax.random.fold_in(_rk, 8), (8,), 0, max(1, 256 // 4) + 1, jnp.int32)
        _ctx_1024P = jax.random.normal(jax.random.fold_in(_rk, 11), (8, 16, 128), jnp.float32)
        _ctx_1024c = jax.random.dirichlet(jax.random.fold_in(_rk, 511), 0.3 * jnp.ones((16,), jnp.float32), (8, 256))
        _ctx_1024t = jnp.einsum('bsk,bkd->bsd', _ctx_1024c, _ctx_1024P)
        _ctx_1024t = _ctx_1024t * jax.lax.rsqrt(jnp.mean(jnp.square(_ctx_1024t)) + 1e-12) * 0.953939
        ctx_1024 = -1.39393e-06 + 0.999914 * (_ctx_1024t + 0.3 * jax.random.normal(jax.random.fold_in(_rk, 611), (8, 256, 128), jnp.float32))
        return (x, ctx_1024)
    x, ctx_1024 = _rec_inputs()

    def _L0_attn_setup():
        import jax, jax.numpy as jnp
        import numpy as np
        D_MODEL = 128
        N_HEADS = 16
        HEAD_DIM = D_MODEL // N_HEADS
        LORA_RANK = 16
        LORA_SCALING = 1.0 / LORA_RANK

        def lora_linear(x, w, a, b):
            return x @ w.T + LORA_SCALING * (x @ a.T @ b.T)
        key = jax.random.key(seed)
        ks = jax.random.split(key, 14)
        B, S = (4, 256)

        def w(k, shape, scale=0.02):
            return jax.random.normal(k, shape, dtype=jnp.float32) * scale
        inp = {'x': jax.random.normal(ks[0], (B, S, D_MODEL), dtype=jnp.float32), 'wq': w(ks[1], (D_MODEL, D_MODEL)), 'aq': w(ks[2], (LORA_RANK, D_MODEL)), 'bq': w(ks[3], (D_MODEL, LORA_RANK)), 'wk': w(ks[4], (D_MODEL, D_MODEL)), 'ak': w(ks[5], (LORA_RANK, D_MODEL)), 'bk': w(ks[6], (D_MODEL, LORA_RANK)), 'wv': w(ks[7], (D_MODEL, D_MODEL)), 'av': w(ks[8], (LORA_RANK, D_MODEL)), 'bv': w(ks[9], (D_MODEL, LORA_RANK)), 'wo': w(ks[10], (D_MODEL, D_MODEL)), 'ao': w(ks[11], (LORA_RANK, D_MODEL)), 'bo': w(ks[12], (D_MODEL, LORA_RANK))}
        return inp
    _L0_attn_all = _L0_attn_setup()
    _L0_attn_in = {k: v for k, v in _L0_attn_all.items() if k in ('wq', 'aq', 'bq', 'wk', 'ak', 'bk', 'wv', 'av', 'bv', 'wo', 'ao', 'bo')}
    del _L0_attn_all

    def _L0_xattn_setup():
        import jax, jax.numpy as jnp
        import numpy as np
        D_MODEL = 128
        NUM_HEADS = 16
        D_HEAD = D_MODEL // NUM_HEADS
        WINDOW = 128

        def _to_heads(x):
            B, S, _ = x.shape
            return x.reshape(B, S, NUM_HEADS, D_HEAD).transpose(0, 2, 1, 3)
        key = jax.random.key(seed)
        ks = jax.random.split(key, 12)
        B, S, D = (2, 256, D_MODEL)
        scale = 1.0 / np.sqrt(D)
        inp = {'query': jax.random.normal(ks[0], (B, S, D), jnp.float32), 'key': jax.random.normal(ks[1], (B, S, D), jnp.float32), 'value': jax.random.normal(ks[2], (B, S, D), jnp.float32), 'Wq': jax.random.normal(ks[3], (D, D), jnp.float32) * scale, 'bq': jnp.zeros((D,), jnp.float32), 'Wk': jax.random.normal(ks[4], (D, D), jnp.float32) * scale, 'bk': jnp.zeros((D,), jnp.float32), 'Wv': jax.random.normal(ks[5], (D, D), jnp.float32) * scale, 'bv': jnp.zeros((D,), jnp.float32), 'Wo': jax.random.normal(ks[6], (D, D), jnp.float32) * scale, 'bo': jnp.zeros((D,), jnp.float32)}
        return inp
    _L0_xattn_all = _L0_xattn_setup()
    _L0_xattn_in = {k: v for k, v in _L0_xattn_all.items() if k in ('Wq', 'bq', 'Wk', 'bk', 'Wv', 'bv', 'Wo', 'bo')}
    del _L0_xattn_all

    def _L0_ffn_setup():
        import jax, jax.numpy as jnp
        import numpy as np
        B, N, C, H, REG = (1, 2309, 128, 16, 5)
        D = C // H
        key = jax.random.key(seed)
        k0, k1, k2, k3 = jax.random.split(key, 4)
        x = jax.random.normal(k0, (B, N, C), dtype=jnp.float32)
        g_info = jax.random.normal(k1, (12, 2, C), dtype=jnp.float32)
        W_qkv = jax.random.normal(k2, (C, 3 * C), dtype=jnp.float32) * 0.02
        W_proj = jax.random.normal(k3, (C, C), dtype=jnp.float32) * 0.02
        b_proj = jnp.zeros((C,), dtype=jnp.float32)
        return {'x': x, 'g_info': g_info, 'W_qkv': W_qkv, 'W_proj': W_proj, 'b_proj': b_proj}
    _L0_ffn_all = _L0_ffn_setup()
    _L0_ffn_in = {k: v for k, v in _L0_ffn_all.items() if k in ('g_info', 'W_qkv', 'W_proj', 'b_proj')}
    del _L0_ffn_all
    return {'x': x, 'ctx_1024': ctx_1024, 'L0_attn_wq': _L0_attn_in['wq'], 'L0_attn_aq': _L0_attn_in['aq'], 'L0_attn_bq': _L0_attn_in['bq'], 'L0_attn_wk': _L0_attn_in['wk'], 'L0_attn_ak': _L0_attn_in['ak'], 'L0_attn_bk': _L0_attn_in['bk'], 'L0_attn_wv': _L0_attn_in['wv'], 'L0_attn_av': _L0_attn_in['av'], 'L0_attn_bv': _L0_attn_in['bv'], 'L0_attn_wo': _L0_attn_in['wo'], 'L0_attn_ao': _L0_attn_in['ao'], 'L0_attn_bo': _L0_attn_in['bo'], 'L0_xattn_Wq': _L0_xattn_in['Wq'], 'L0_xattn_bq': _L0_xattn_in['bq'], 'L0_xattn_Wk': _L0_xattn_in['Wk'], 'L0_xattn_bk': _L0_xattn_in['bk'], 'L0_xattn_Wv': _L0_xattn_in['Wv'], 'L0_xattn_bv': _L0_xattn_in['bv'], 'L0_xattn_Wo': _L0_xattn_in['Wo'], 'L0_xattn_bo': _L0_xattn_in['bo'], 'L0_ffn_g_info': _L0_ffn_in['g_info'], 'L0_ffn_W_qkv': _L0_ffn_in['W_qkv'], 'L0_ffn_W_proj': _L0_ffn_in['W_proj'], 'L0_ffn_b_proj': _L0_ffn_in['b_proj']}

def reference(x, ctx_1024, L0_attn_wq, L0_attn_aq, L0_attn_bq, L0_attn_wk, L0_attn_ak, L0_attn_bk, L0_attn_wv, L0_attn_av, L0_attn_bv, L0_attn_wo, L0_attn_ao, L0_attn_bo, L0_xattn_Wq, L0_xattn_bq, L0_xattn_Wk, L0_xattn_bk, L0_xattn_Wv, L0_xattn_bv, L0_xattn_Wo, L0_xattn_bo, L0_ffn_g_info, L0_ffn_W_qkv, L0_ffn_W_proj, L0_ffn_b_proj):
    import jax
    import jax.numpy as jnp

    def _L0_attn_ref(x, wq, aq, bq, wk, ak, bk, wv, av, bv, wo, ao, bo):
        import jax, jax.numpy as jnp
        import numpy as np
        D_MODEL = 128
        N_HEADS = 16
        HEAD_DIM = D_MODEL // N_HEADS
        LORA_RANK = 16
        LORA_SCALING = 1.0 / LORA_RANK

        def lora_linear(x, w, a, b):
            return x @ w.T + LORA_SCALING * (x @ a.T @ b.T)
        B, S, _ = x.shape

        def split_heads(t):
            return t.reshape(B, S, N_HEADS, HEAD_DIM).transpose(0, 2, 1, 3)
        q = split_heads(lora_linear(x, wq, aq, bq))
        k = split_heads(lora_linear(x, wk, ak, bk))
        v = split_heads(lora_linear(x, wv, av, bv))
        scores = jnp.einsum('bhqd,bhkd->bhqk', q, k) / jnp.sqrt(jnp.float32(HEAD_DIM))
        causal = jnp.tril(jnp.ones((S, S), dtype=bool))
        scores = jnp.where(causal, scores, -jnp.inf)
        attn = jax.nn.softmax(scores, axis=-1)
        ctx = jnp.einsum('bhqk,bhkd->bhqd', attn, v)
        ctx = ctx.transpose(0, 2, 1, 3).reshape(B, S, D_MODEL)
        return lora_linear(ctx, wo, ao, bo)

    def _L0_xattn_ref(query, key, value, Wq, bq, Wk, bk, Wv, bv, Wo, bo):
        import jax, jax.numpy as jnp
        import numpy as np
        D_MODEL = 128
        NUM_HEADS = 16
        D_HEAD = D_MODEL // NUM_HEADS
        WINDOW = 128

        def _to_heads(x):
            B, S, _ = x.shape
            return x.reshape(B, S, NUM_HEADS, D_HEAD).transpose(0, 2, 1, 3)
        B, S, D = query.shape
        q = _to_heads(query @ Wq + bq)
        k = _to_heads(key @ Wk + bk)
        v = _to_heads(value @ Wv + bv)
        scores = jnp.einsum('bhqd,bhkd->bhqk', q, k) / jnp.sqrt(jnp.float32(D_HEAD))
        i = jnp.arange(S)[:, None]
        j = jnp.arange(S)[None, :]
        local_mask = jnp.abs(i - j) <= WINDOW // 2
        scores = jnp.where(local_mask[None, None], scores, -jnp.inf)
        attn = jax.nn.softmax(scores, axis=-1)
        ctx = jnp.einsum('bhqk,bhkd->bhqd', attn, v)
        ctx = ctx.transpose(0, 2, 1, 3).reshape(B, S, D)
        return ctx @ Wo + bo

    def _L0_ffn_ref(x, g_info, W_qkv, W_proj, b_proj):
        import jax, jax.numpy as jnp
        import numpy as np
        B, N, C, H, REG = (1, 2309, 128, 16, 5)
        D = C // H
        Bx, Nx, Cx = x.shape
        scale = D ** (-0.5)
        qkv = (x @ W_qkv).reshape(Bx, Nx, 3, H, D)
        q, k, v = (qkv[:, :, 0], qkv[:, :, 1], qkv[:, :, 2])
        g_layer = g_info[0].reshape(-1, H, D)
        q_g = g_layer[0]
        q_pure = q[:, REG:]
        q_n = q_pure / jnp.linalg.norm(q_pure, axis=-1, keepdims=True)
        qg_n = q_g / jnp.linalg.norm(q_g, axis=-1, keepdims=True)
        sim = (qg_n[None, None] * q_n).sum(-1).mean(-1)
        sim = (sim - sim.min()) / (sim.max() - sim.min())
        pos = sim > 0.9
        logits = jnp.einsum('bqhd,bkhd->bhqk', q * scale, k)

        def masked_attn(tok_mask):
            key_mask = jnp.concatenate([jnp.ones((Bx, REG), bool), tok_mask], axis=1)
            l = jnp.where(key_mask[:, None, None, :], logits, -jnp.inf)
            a = jax.nn.softmax(l, axis=-1)
            return jnp.einsum('bhqk,bkhd->bqhd', a, v)
        x_pos = masked_attn(pos)
        x_neg = masked_attn(~pos)
        reg_out = (x_pos[:, :REG] + x_neg[:, :REG]) * 0.5
        tok_out = jnp.where(pos[:, :, None, None], x_pos[:, REG:], x_neg[:, REG:])
        out = jnp.concatenate([reg_out, tok_out], axis=1).reshape(Bx, Nx, Cx)
        return out @ W_proj + b_proj
    x = x + _L0_attn_ref(_layernorm(x, axis=-1), L0_attn_wq, L0_attn_aq, L0_attn_bq, L0_attn_wk, L0_attn_ak, L0_attn_bk, L0_attn_wv, L0_attn_av, L0_attn_bv, L0_attn_wo, L0_attn_ao, L0_attn_bo)
    x = x + _L0_xattn_ref(_layernorm(x, axis=-1), ctx_1024, ctx_1024, L0_xattn_Wq, L0_xattn_bq, L0_xattn_Wk, L0_xattn_bk, L0_xattn_Wv, L0_xattn_bv, L0_xattn_Wo, L0_xattn_bo)
    x = x + _L0_ffn_ref(_layernorm(x, axis=-1), L0_ffn_g_info, L0_ffn_W_qkv, L0_ffn_W_proj, L0_ffn_b_proj)
    return x

_drawn_inputs = setup_inputs


def setup_inputs(seed=0):
    import zlib

    import numpy as np

    out = dict(_drawn_inputs(seed))
    spreads = {'L0_xattn_bq': (0.0, 0.347),
     'L0_xattn_bk': (0.0, 0.8),
     'L0_xattn_bv': (0.0, 0.1),
     'L0_xattn_bo': (0.0, 0.1),
     'L0_ffn_b_proj': (0.0, 0.1)}
    factors = {'L0_attn_wq': 8.0,
     'L0_attn_aq': 8.0,
     'L0_attn_bq': 8.0,
     'L0_attn_wk': 8.0,
     'L0_attn_ak': 8.0,
     'L0_attn_bk': 8.0,
     'L0_attn_wv': 8.0,
     'L0_attn_av': 8.0,
     'L0_attn_bv': 8.0,
     'L0_attn_wo': 8.0,
     'L0_attn_ao': 8.0,
     'L0_attn_bo': 8.0,
     'L0_ffn_g_info': 8.0,
     'L0_ffn_W_qkv': 2.827,
     'L0_ffn_W_proj': 2.749}
    for name, (base, spread) in spreads.items():
        noise = np.random.default_rng([zlib.crc32(name.encode()), seed]).standard_normal(out[name].shape)
        drawn = base * np.exp(spread * noise) if base else spread * noise
        out[name] = jnp.asarray(drawn.astype(out[name].dtype))
    for name, factor in factors.items():
        out[name] = (out[name] * factor).astype(out[name].dtype)
    return out
```

```python
from contextlib import ExitStack

import concourse.bass as bass
from concourse import mybir

F32 = mybir.dt.float32
BF16 = mybir.dt.bfloat16
ALU = mybir.AluOpType
ACT = mybir.ActivationFunctionType
AX = mybir.AxisListType
RMAX = bass.bass_isa.ReduceOp.max

SELF, CROSS, CLASS, IDLE = "self", "cross", "class", "idle"
Q, K, V_, O = range(4)
MASKED = -1.0e30
EPS = 1e-5
SIM_CUT = 0.9
REG = 5

TERMS = [(0, 0), (0, 1), (0, 2), (1, 0), (1, 1), (2, 0)]


def layer_kernel(nc: bass.Bass, x, ctx_1024, L0_attn_wq, L0_attn_aq, L0_attn_bq, L0_attn_wk, L0_attn_ak,
                 L0_attn_bk, L0_attn_wv, L0_attn_av, L0_attn_bv, L0_attn_wo, L0_attn_ao, L0_attn_bo,
                 L0_xattn_Wq, L0_xattn_bq, L0_xattn_Wk, L0_xattn_bk, L0_xattn_Wv, L0_xattn_bv, L0_xattn_Wo,
                 L0_xattn_bo, L0_ffn_g_info, L0_ffn_W_qkv, L0_ffn_W_proj, L0_ffn_b_proj, out):
    B, S, D = x.shape
    RANK = L0_attn_aq.shape[0]
    NH = 16
    HD = D // NH
    P = 128
    NT = S // P
    HH = NH // 2
    WIN = 64
    WW = P + WIN
    NTERM = len(TERMS)
    CLS = HD * NTERM
    MROW = 96
    KA = MROW
    KB = MROW + 3
    SCALE = float(HD) ** -0.5
    GV = 4 * 32
    XC = 8
    assert D == P and S == 2 * P and HD == 8

    UNITS = ([(SELF, b) for b in range(B)] + [(CROSS, b) for b in range(B)] + [(IDLE, 0)] * 2
             + [(CLASS, b) for b in range(B)])
    CROSS0, CLASS0, NU = B, 2 * B + 2, len(UNITS)

    def kind(u):
        return UNITS[u][0] if 0 <= u < NU else IDLE

    def live(u):
        return kind(u) != IDLE

    STG = {SELF: 0, CROSS: 1, CLASS: 2}

    def bench_tasks(g, p):
        n, h = g // 2, g % 2
        t = []
        if p == 1 and live((g + 1) // 2):
            t.append(("max_rows", g + 1))
        if p == 3 and kind(n) == CLASS:
            t.append(("reg_scores", g))
        if p == 7 and kind(n) == CLASS:
            t.append(("reg_values", g))
        if p == 3 and g >= 1 and kind((g - 1) // 2) == CLASS:
            t.append(("reg_turn", g - 1))
        if h == 0:
            u = n + 2
            if p == 2 and kind(u) in (SELF, CROSS):
                t.append(("turn_x", u))
            if p == 3 and kind(u) == CROSS:
                t.append(("turn_ctx", u))
            if p == 3 and kind(u) in (SELF, CROSS):
                t.append(("qk", u))
            if p == 4 and live(n - 1):
                t.append(("turn_out", g - 1))
            if p == 5 and live(n - 1):
                t.append(("turn_heads", n - 1))
            if p == 6 and live(n - 1):
                t.append(("project", n - 1))
        else:
            if p == 1 and kind(n - 1) == CROSS:
                t.append(("turn_x3", n - 1))
            if p == 2 and kind(n - 1) == CROSS:
                t.append(("qk3", n - 1))
            if p == 3 and kind(n - 1) == CROSS:
                t.append(("q_tokens", n - 1))
            if p == 4 and live(n):
                t.append(("turn_out", g - 1))
            if p == 5 and live(n + 1):
                t.append(("values", n + 1))
            if p == 7 and n == CLASS0 - 2:
                t.append(("turn_class", 0))
        return t

    FIRST, LAST = -5, 2 * NU + 2
    SLOTS = range(FIRST, LAST)
    SETUP_TASKS = [("lora_turn", 0), ("lora_merge", 0)]
    bench_order, norm_order, part_order = {}, {}, {}
    for task in SETUP_TASKS:
        bench_order[task] = len(bench_order)
    for g in SLOTS:
        for p in range(8):
            for task in bench_tasks(g, p):
                bench_order[task] = len(bench_order)

    def norm_tasks(g, p):
        n, h = g // 2, g % 2
        t = []
        if h == 1 and kind(n + 3) in (SELF, CROSS):
            if p == 5:
                t.append(("stats", n + 3))
            if p == 7:
                t.append(("scale", n + 3))
        if kind(n - 1) == CROSS:
            if h == 0 and p == 7:
                t.append(("stats", n - 1 + B + 2 + NU))
            if h == 1 and p == 0:
                t.append(("scale", n - 1 + B + 2 + NU))
        return t

    for g in SLOTS:
        for p in range(8):
            for what, u in norm_tasks(g, p):
                if what == "stats":
                    norm_order[u] = len(norm_order)
            for what, u in bench_tasks(g, p):
                if what in ("qk", "qk3"):
                    part_order[u + (B + 2 if what == "qk3" else 0)] = len(part_order)

    def turn(task, u):
        return bench_order[(task, u)]

    def max_chunks(g):
        if g < 0:
            return []
        k = kind(g // 2)
        if k == SELF:
            return ([("tile0", 4 * i) for i in range(HH // 4)] + [("tile1", 2 * i) for i in range(HH // 2)])
        if k == CROSS:
            return [("window", i) for i in range(HH)]
        if k == CLASS:
            return [("full", i) for i in range(HH)] + [("reg", 0)]
        return []

    chunk_base = {}
    total = 0
    for g in range(0, 2 * NU):
        chunk_base[g] = total
        total += len(max_chunks(g))

    def max_part(g, p):
        c = max_chunks(g)
        lo, hi = len(c) * (p // 2) // 4, len(c) * (p // 2 + 1) // 4
        return [(i, c[i]) for i in range(lo, hi)]

    live_halves = [g for g in range(2 * NU) if live(g // 2)]
    half_no = {g: i for i, g in enumerate(live_halves)}
    unit_no = {u: half_no[2 * u] // 2 for u in range(NU) if live(u)}
    NCHB = HH // 2
    WIDTH = {SELF: S + P, CROSS: 2 * WW, CLASS: 2 * S}

    with ExitStack() as ctx:
        def sb(name, shape, dt=F32):
            return ctx.enter_context(nc.sbuf_tensor(name, shape, dt))

        def sem(name):
            return ctx.enter_context(nc.semaphore(name))

        xr = sb("xr", [P, B, NT, D])
        ct = sb("ct", [P, B, NT, D])
        w = sb("w", [P, 3, 4, D])
        wraw = sb("wraw", [P, 4, D])
        lo_a = sb("lo_a", [RANK, 4, D])
        lo_b = sb("lo_b", [P, 4, RANK])
        lo_bt = sb("lo_bt", [RANK, 4, D])
        qk_bias = sb("qk_bias", [P, 2])
        v_bias = sb("v_bias", [P, D])
        o_bias = sb("o_bias", [P, 2, D])
        g_row = sb("g_row", [P, D])
        g_sq = sb("g_sq", [P, D])
        g_n2 = sb("g_n2", [P, NH])
        g_rn = sb("g_rn", [P, NH])
        g_hat = sb("g_hat", [P, D])
        ident = sb("ident", [P, P])
        identb = sb("identb", [P, P], BF16)
        mask_c = sb("mask_c", [P, 4, P], BF16)
        mask_w = sb("mask_w", [P, NT, WW], BF16)
        neg_half = sb("neg_half", [P, NT * NH])
        qs = sb("qs", [P, 2, NH, S], BF16)
        ks = sb("ks", [P, 2, NH, S], BF16)
        qx = sb("qx", [P, 2, NH, 32], BF16)
        qx_cls = sb("qx_cls", [1, 2, 2, NH, 32], BF16)
        pr = sb("pr", [P, 4, 2, 2 * S])
        vv = sb("vv", [P, 2, NT, NH, 32])
        ot = sb("ot", [P, 2, 2, S])
        heads = sb("heads", [P, NT, D])
        heads_t = sb("heads_t", [P, S])
        rec = sb("rec", [P, NT * HH])
        st6 = sb("st6", [P, NT, 6])
        mv = sb("mv", [P, NT, 2])
        ve = sb("ve", [P, NT])
        rs = sb("rs", [P, NT])
        xn = sb("xn", [P, NT, D])
        xt = sb("xt", [P, 2, S])
        cx = sb("cx", [P, 2, S])
        xt3 = sb("xt3", [P, B, S])
        rest = sb("rest", [P, 2, S])
        parts = sb("parts", [P, 3, 2, S], BF16)
        nm = sb("nm", [P, 2, NT, HH])
        nmr = sb("nmr", [P, NT, HH])
        mp = sb("mp", [P, 2, NT, 3, HH], BF16)
        mt = sb("mt", [3 * HH, 2, S], BF16)
        nx = sb("nx", [P, 2, 2])
        nxr = sb("nxr", [P, 2])
        mpx = sb("mpx", [P, 2, 3, 2], BF16)
        mtx = sb("mtx", [6, 2, P], BF16)
        px = sb("px", [P, HH, NT, XC])
        otx = sb("otx", [P, 2, XC])
        recx = sb("recx", [XC, HH])
        hx = sb("hx", [XC, 2, HH * HD])
        sq = sb("sq", [P, NT * D])
        dg = sb("dg", [P, NT * D])
        n2 = sb("n2", [P, B, NT * NH])
        dq = sb("dq", [P, B, NT * NH])
        rn = sb("rn", [P, B, NT * NH])
        sh = sb("sh", [P, B, NT * NH])
        sim = sb("sim", [P, 3, B, NT])
        ends = sb("ends", [P, 2])
        ends_all = sb("ends_all", [P, 2])
        span = sb("span", [P, 2])
        pos = sb("pos", [P, B, NT])
        cls = sb("cls", [P, 4, B, NT], BF16)
        cls_t = sb("cls_t", [4 * B * NT, P], BF16)

        ps_a = ctx.enter_context(nc.psum_tensor("ps_a", [P, 2, 512], F32))
        ps_b = ctx.enter_context(nc.psum_tensor("ps_b", [P, 2, 2, 512], F32))
        ps_v = ctx.enter_context(nc.psum_tensor("ps_v", [P, 2, S], F32))
        bench = ctx.enter_context(nc.psum_tensor("bench", [P, 512], F32))
        bench16 = bench[:, :].bitcast(BF16)

        part_scr = nc.dram_tensor("part_scr", (NU, P, 3, 2, S), BF16).ap()
        max_scr = nc.dram_tensor("max_scr", (2 * NU, 3 * HH, S), BF16).ap()
        maxx_scr = nc.dram_tensor("maxx_scr", (2 * NU, 6, P), BF16).ap()
        cls_scr = nc.dram_tensor("cls_scr", (4, B * NT, P), BF16).ap()

        x_first, x_rest, ctx_in, w_lora, w_in, small_in = map(
            sem, ["x_first", "x_rest", "ctx_in", "w_lora", "w_in", "small_in"])
        ident_made, consts_made, stacks_zero, qx_made, g_pow = map(
            sem, ["ident_made", "consts_made", "stacks_zero", "qx_made", "g_pow"])
        pool_step, dve_step = sem("pool_step"), sem("dve_step")
        filled = sem("filled")
        cleared = sem("cleared")
        stats_ready, rstd_ready, xn_ready = map(sem, ["stats_ready", "rstd_ready", "xn_ready"])
        bias_added = sem("bias_added")
        part1_ready, part2_ready, parts_ready = map(sem, ["part1_ready", "part2_ready", "parts_ready"])
        parts_stored = sem("parts_stored")
        stack_ready = [sem(f"stack_ready{i}") for i in range(4)]
        qx_ready = sem("qx_ready")
        max_scores, max_taken, max_parts = map(sem, ["max_scores", "max_taken", "max_parts"])
        max_stored = sem("max_stored")
        max_ready = [sem("max_ready0"), sem("max_ready1")]
        scores, exp_done, masked = map(sem, ["scores", "exp_done", "masked"])
        pv_done, ot_ready = sem("pv_done"), sem("ot_ready")
        sq_ready, stats3_ready, rn_ready = map(sem, ["sq_ready", "stats3_ready", "rn_ready"])
        ends_ready, ends_done, cls_ready, cls_stored = map(
            sem, ["ends_ready", "ends_done", "cls_ready", "cls_stored"])
        stored = sem("stored")

        def stack_sem(g):
            return stack_ready[g % 4]

        def stack_count(g):
            total = 0
            for gg in range(g % 4, g + 1, 4):
                if live(gg // 2):
                    total += 16 * (2 * NTERM + (2 if kind(gg // 2) == CLASS else 0))
            return total

        def max_count(g):
            total = 0
            for gg in range(g % 2, g + 1, 2):
                if live(gg // 2):
                    total += 16 * (2 if kind(gg // 2) == CLASS else 1)
            return total

        CLASS_HALVES = [g for g in live_halves if kind(g // 2) == CLASS]
        def class_no(g):
            return CLASS_HALVES.index(g)

        def max_store_count(g):
            return 16 * sum(2 if kind(gg // 2) == CLASS else 1 for gg in live_halves if gg <= g)

        def bias_count(u):
            return sum(1 for v, i in norm_order.items() if i <= norm_order[u] and (v >= NU or kind(v) == CROSS))

        block = ctx.enter_context(nc.Block())

        @block.sync
        def _(sp):
            def rows(v):
                return v.rearrange("(a n) -> a n", a=1)

            sp.dma_start(xr[:, 0], x[0].rearrange("(t p) d -> p t d", p=P)).then_inc(x_first, 16)
            for i, a in enumerate((L0_attn_wq, L0_attn_wk, L0_attn_wv, L0_attn_wo)):
                sp.dma_start(wraw[:, i, :], a).then_inc(w_lora, 16)
            for i, a in enumerate((L0_attn_aq, L0_attn_ak, L0_attn_av, L0_attn_ao)):
                sp.dma_start(lo_a[:, i, :], a).then_inc(w_lora, 16)
            for i, a in enumerate((L0_attn_bq, L0_attn_bk, L0_attn_bv, L0_attn_bo)):
                sp.dma_start(lo_b[:, i, :], a).then_inc(w_lora, 16)
            for b in range(1, B):
                sp.dma_start(xr[:, b], x[b].rearrange("(t p) d -> p t d", p=P)).then_inc(x_rest, 16)

            def stacks(g):
                u, h0, buf = g // 2, HH * (g % 2), (g // 2) % 2
                sp.wait_ge(parts_stored, 16 * (part_order[u] + 1))
                if g - 4 >= 0 and live((g - 4) // 2):
                    sp.wait_ge(scores, NCHB * (half_no[g - 4] + 1))
                if g < 4:
                    sp.wait_ge(stacks_zero, 3)
                src = part_scr[u].rearrange("(h d) a s q -> d h a s q", d=HD)
                for t, (a, b) in enumerate(TERMS):
                    r = slice(HD * t, HD * (t + 1))
                    sp.dma_start(qs[r, buf, h0:h0 + HH, :], src[:, h0:h0 + HH, a, 0, :]).then_inc(stack_sem(g), 16)
                    sp.dma_start(ks[r, buf, h0:h0 + HH, :], src[:, h0:h0 + HH, b, 1, :]).then_inc(stack_sem(g), 16)
                if kind(u) == CLASS:
                    sp.wait_ge(cls_stored, 16)
                    if g - 4 >= 0 and kind((g - 4) // 2) == CLASS:
                        sp.wait_ge(filled, turn("reg_scores", g - 4) + 1)
                    bb = UNITS[u][1]
                    for s, dst in ((0, qs), (2, ks)):
                        c = cls_scr[s:s + 2, NT * bb:NT * bb + NT, :].rearrange("k t q -> k (t q)")
                        c = c.unsqueeze(1).broadcast_to([2, HH, S])
                        sp.dma_start(dst[CLS:CLS + 2, buf, h0:h0 + HH, :], c).then_inc(stack_sem(g), 16)

            def max_rows(g):
                u, h0, buf = g // 2, HH * (g % 2), (g // 2) % 2
                sp.wait_ge(cleared, turn("max_rows", g) + 1)
                sp.dma_start(max_scr[g], mt[:, g % 2, :]).then_inc(max_stored, 16)
                if kind(u) == CLASS:
                    sp.dma_start(maxx_scr[g], mtx[:, g % 2, :]).then_inc(max_stored, 16)
                sp.wait_ge(max_stored, max_store_count(g))
                sp.dma_start(qs[MROW:MROW + 3, buf, h0:h0 + HH, :],
                             max_scr[g].rearrange("(k h) q -> k h q", k=3)).then_inc(max_ready[g % 2], 16)
                if kind(u) == CLASS:
                    c = maxx_scr[g].rearrange("(k g) c -> k (g c)", k=3).rearrange("k (h r) -> k h r", h=HH)
                    sp.dma_start(qx[MROW:MROW + 3, buf, h0:h0 + HH, :], c).then_inc(max_ready[g % 2], 16)

            def store_parts(u):
                sp.wait_ge(parts_ready, part_order[u] + 1)
                sp.dma_start(part_scr[u], parts[:, :, :, :]).then_inc(parts_stored, 16)

            def finish(b):
                sp.wait_ge(cleared, turn("project", CLASS0 + b) + 1)
                sp.dma_start(out[b].rearrange("(t p) d -> p t d", p=P), xr[:, b]).then_inc(stored, 16)

            sent_rest = False
            for g in SLOTS:
                n, h = g // 2, g % 2
                if g == -3:
                    for b in range(B):
                        sp.dma_start(ct[:, b], ctx_1024[b].rearrange("(t p) d -> p t d", p=P)).then_inc(ctx_in, 16)
                    for i, a in enumerate((L0_xattn_Wq, L0_xattn_Wk, L0_xattn_Wv, L0_xattn_Wo)):
                        sp.dma_start(w[:, 1, i, :], a).then_inc(w_in, 16)
                    sp.dma_start(w[:, 2, 0:3, :], L0_ffn_W_qkv.rearrange("i (a o) -> i a o", a=3)).then_inc(w_in, 16)
                    sp.dma_start(w[:, 2, 3, :], L0_ffn_W_proj).then_inc(w_in, 16)
                    for i, a in enumerate((L0_xattn_bq, L0_xattn_bk)):
                        sp.dma_start(qk_bias[:, i:i + 1], a.rearrange("(p a) -> p a", a=1)).then_inc(small_in, 16)
                    for dst, a in ((v_bias[:, :], rows(L0_xattn_bv)), (o_bias[:, 0, :], rows(L0_xattn_bo)),
                                   (o_bias[:, 1, :], rows(L0_ffn_b_proj)),
                                   (g_row[:, :], L0_ffn_g_info[0, 0:1, :])):
                        sp.dma_start(dst, a.broadcast_to([P, D])).then_inc(small_in, 16)
                    sp.wait_ge(qx_made, 2)
                    for k in range(2):
                        sp.dma_start(qx[CLS + k:CLS + k + 1], qx_cls[0:1, k]).then_inc(small_in, 16)
                if 0 <= g + 3 and live((g + 3) // 2) and kind((g + 3) // 2) != CLASS:
                    stacks(g + 3)
                if live((g + 1) // 2):
                    max_rows(g + 1)
                if n == CLASS0 - 2 and h == 1:
                    sp.wait_ge(cleared, turn("turn_class", 0) + 1)
                    sp.dma_start(cls_scr.rearrange("k t q -> (k t) q"), cls_t[:, :]).then_inc(cls_stored, 16)
                    stacks(2 * CLASS0)
                    stacks(2 * CLASS0 + 1)
                elif kind((g + 3) // 2) == CLASS and g + 3 > 2 * CLASS0 + 1:
                    stacks(g + 3)
                if h == 0 and kind(n + 2) in (SELF, CROSS):
                    store_parts(n + 2)
                if h == 1 and kind(n - 1) == CROSS:
                    store_parts(n - 1 + B + 2)
                if h == 1 and kind(n - 1) == CLASS:
                    finish(UNITS[n - 1][1])
            sp.wait_ge(stored, 16 * B)
            sp.wait_ge(parts_stored, 16 * 3 * B)
            sp.wait_ge(max_stored, max_store_count(2 * NU))

        @block.tensor
        def _(pe):
            def begin(task, u):
                if turn(task, u) > 0:
                    pe.wait_ge(cleared, turn(task, u))

            def second_pass(g, c):
                u, buf, h0 = g // 2, (g // 2) % 2, HH * (g % 2)
                i = NCHB * half_no[g] + c
                if c == 0:
                    pe.wait_ge(max_ready[g % 2], max_count(g))
                if i >= 2:
                    pe.wait_ge(exp_done, i - 1)
                for j in range(2):
                    h = h0 + 2 * c + j
                    bank = ps_b[:, i % 2, j, :]
                    if kind(u) == SELF:
                        spans = ((0, 0, S), (1, P, S))
                    elif kind(u) == CROSS:
                        spans = ((0, 0, WW), (1, S - WW, S))
                    else:
                        spans = ((0, 0, S), (1, 0, S))
                    at = 0
                    for t, a, b in spans:
                        last = pe.matmul(bank[:, at:at + b - a], ks[0:KB, buf, h, t * P:(t + 1) * P],
                                         qs[0:KB, buf, h, a:b], start=True, stop=True)
                        at += b - a
                last.then_inc(scores, 1)

            def first_pass(g, i, chunk):
                what, h1 = chunk
                u, buf, h0 = g // 2, (g // 2) % 2, HH * (g % 2)
                no = chunk_base[g] + i
                if i == 0:
                    pe.wait_ge(stack_sem(g), stack_count(g))
                if what == "reg":
                    pe.wait_ge(qx_ready, class_no(g) + 1)
                if no >= 2:
                    pe.wait_ge(max_taken, no - 1)
                bank = ps_a[:, no % 2, :]

                def part(dst, h, t, a, b, start):
                    return pe.matmul(dst, qs[0:KA, buf, h, t * P:(t + 1) * P], ks[0:KA, buf, h, a:b],
                                     start=start, stop=True, skip_group_check=True)

                if what == "tile0":
                    pe.matmul(bank, identb[:, :], mask_c[:, :, :].rearrange("p a b -> p (a b)"),
                              start=True, stop=False, skip_group_check=True)
                    for j in range(4):
                        last = part(bank[:, P * j:P * (j + 1)], h0 + h1 + j, 0, 0, P, False)
                elif what == "tile1":
                    pe.matmul(bank.rearrange("p (a b) -> p a b", a=2)[:, :, P:S], identb[:, :], mask_c[:, 0:2, :],
                              start=True, stop=False, skip_group_check=True)
                    for j in range(2):
                        last = part(bank[:, S * j:S * (j + 1)], h0 + h1 + j, 1, 0, S, False)
                elif what == "window":
                    pe.matmul(bank[:, 0:2 * WW], identb[:, :], mask_w[:, :, :].rearrange("p a b -> p (a b)"),
                              start=True, stop=False, skip_group_check=True)
                    for t in range(NT):
                        a = t * (S - WW)
                        last = part(bank[:, WW * t:WW * (t + 1)], h0 + h1, t, a, a + WW, False)
                elif what == "full":
                    for t in range(NT):
                        last = part(bank[:, S * t:S * (t + 1)], h0 + h1, t, 0, S, True)
                else:
                    for j in range(4):
                        for q in range(2):
                            last = pe.matmul(bank[32 * j:32 * j + 32, S * q:S * (q + 1)],
                                             qx[0:KA, buf, h0 + 4 * q + j, :], ks[0:KA, buf, h0 + 4 * q + j, :],
                                             start=True, stop=True, skip_group_check=True)
                last.then_inc(max_scores, 1)

            def values_pass(g, quad):
                u, buf = g // 2, (g // 2) % 2
                i = NCHB * half_no[g] + 2 * quad
                if kind(u) == CLASS:
                    pe.wait_ge(exp_done, i + 2)
                else:
                    pe.wait_ge(masked, i + 2)
                if quad == 0:
                    pe.wait_ge(cleared, turn("values", u) + 1)
                    if half_no[g] > 0:
                        pe.wait_ge(ot_ready, half_no[g])
                for t in range(NT):
                    for j in range(4):
                        h = HH * (g % 2) + 4 * quad + j
                        p = pr[:, (i + j // 2) % 4, j % 2, :]
                        if kind(u) == SELF:
                            a, b, at = ((0, S, 0), (P, S, S))[t]
                        elif kind(u) == CROSS:
                            a, b, at = ((0, WW, 0), (S - WW, S, WW))[t]
                        else:
                            a, b, at = ((0, S, 0), (0, S, S))[t]
                        last = pe.matmul(ps_v[32 * j:32 * j + 32, quad, a:b], vv[:, buf, t, h, :],
                                         p[:, at:at + b - a], start=(t == 0), stop=True, skip_group_check=True)
                last.then_inc(pv_done, 1)

            def run(task, u):
                begin(task, u)
                if task == "lora_turn":
                    pe.wait_ge(w_lora, 16 * 12)
                    pe.wait_ge(ident_made, 2)
                    for i in range(4):
                        last = pe.transpose(bench[0:RANK, D * i:D * (i + 1)], lo_b[:, i, :], ident[:, :])
                elif task == "lora_merge":
                    pe.wait_ge(cleared, turn("lora_turn", 0) + 1)
                    for i in range(4):
                        pe.matmul(bench[:, D * i:D * (i + 1)], wraw[:, i, :], ident[:, :],
                                  start=True, stop=False, skip_group_check=True)
                        last = pe.matmul(bench[:, D * i:D * (i + 1)], lo_a[:, i, :], lo_bt[:, i, :],
                                         start=False, stop=True, skip_group_check=True)
                elif task == "max_rows":
                    g = u
                    pe.wait_ge(max_parts, half_no[g] + 1)
                    for t in range(NT):
                        last = pe.transpose(bench16[0:3 * HH, P * t:P * (t + 1)],
                                            mp[:, g % 2, t].rearrange("p k h -> p (k h)"), identb[:, :])
                    if kind(g // 2) == CLASS:
                        last = pe.transpose(bench16[0:6, S:S + P], mpx[:, g % 2].rearrange("p k q -> p (k q)"),
                                            identb[:, :])
                elif task in ("turn_x", "turn_x3"):
                    v = u if task == "turn_x" else u + B + 2 + NU
                    pe.wait_ge(xn_ready, norm_order[v] + 1)
                    for t in range(NT):
                        last = pe.transpose(bench[:, P * t:P * (t + 1)], xn[:, t, :], ident[:, :])
                elif task == "turn_ctx":
                    pe.wait_ge(ctx_in, 16 * B)
                    for t in range(NT):
                        last = pe.transpose(bench[:, P * t:P * (t + 1)], ct[:, UNITS[u][1], t, :], ident[:, :])
                elif task in ("qk", "qk3"):
                    if task == "qk":
                        st, xq = STG[kind(u)], xt[:, u % 2, :]
                        xk = cx[:, u % 2, :] if kind(u) == CROSS else xq
                        pe.wait_ge(cleared, turn("turn_ctx" if kind(u) == CROSS else "turn_x", u) + 1)
                    else:
                        st, xq = 2, xt3[:, UNITS[u][1], :]
                        xk = xq
                        pe.wait_ge(cleared, turn("turn_x3", u) + 1)
                    if st:
                        pe.wait_ge(w_in, 16 * 6)
                    pe.matmul(bench[:, 0:S], w[:, st, Q, :], xq, start=True, stop=True)
                    last = pe.matmul(bench[:, S:2 * S], w[:, st, K, :], xk, start=True, stop=True)
                elif task == "q_tokens":
                    for t in range(NT):
                        last = pe.matmul(bench[:, P * t:P * (t + 1)], xt3[:, UNITS[u][1], P * t:P * (t + 1)],
                                         w[:, 2, Q, :], start=True, stop=True)
                elif task == "values":
                    k, b = UNITS[u]
                    src = {SELF: xt[:, u % 2, :], CROSS: cx[:, u % 2, :], CLASS: xt3[:, b, :]}[k]
                    for t in range(NT):
                        last = pe.matmul(bench[:, P * t:P * (t + 1)], src[:, P * t:P * (t + 1)],
                                         w[:, STG[k], V_, :], start=True, stop=True)
                elif task == "turn_out":
                    g = u
                    pe.wait_ge(ot_ready, half_no[g] + 1)
                    for t in range(NT):
                        for q in range(2):
                            i = 2 * t + q
                            last = pe.transpose(bench[:, GV * i:GV * (i + 1)], ot[:, g % 2, q, P * t:P * (t + 1)],
                                                ident[:, :])
                elif task == "turn_heads":
                    for t in range(NT):
                        last = pe.transpose(bench[:, P * t:P * (t + 1)], heads[:, t, :], ident[:, :])
                elif task == "project":
                    for t in range(NT):
                        last = pe.matmul(bench[:, P * t:P * (t + 1)], heads_t[:, P * t:P * (t + 1)],
                                         w[:, STG[kind(u)], O, :], start=True, stop=True)
                elif task == "reg_scores":
                    g = u
                    buf, h0 = (g // 2) % 2, HH * (g % 2)
                    for h in range(HH):
                        for t in range(NT):
                            i = NT * h + t
                            last = pe.matmul(bench[:, XC * i:XC * (i + 1)], ks[0:KB, buf, h0 + h, P * t:P * (t + 1)],
                                             qx[0:KB, buf, h0 + h, 0:XC], start=True, stop=True)
                elif task == "reg_values":
                    g = u
                    buf, h0 = (g // 2) % 2, HH * (g % 2)
                    for q in range(2):
                        for t in range(NT):
                            for j in range(4):
                                last = pe.matmul(bench[32 * j:32 * j + 32, XC * q:XC * (q + 1)],
                                                 vv[:, buf, t, h0 + 4 * q + j, :], px[:, 4 * q + j, t, :],
                                                 start=(t == 0), stop=True, skip_group_check=True)
                elif task == "reg_turn":
                    for q in range(2):
                        last = pe.transpose(bench[0:XC, GV * q:GV * (q + 1)], otx[:, q, :], ident[:, :])
                elif task == "turn_class":
                    pe.wait_ge(cls_ready, 1)
                    last = pe.transpose(bench16[0:4 * B * NT, 0:P], cls[:, :, :, :].rearrange("p k b t -> p (k b t)"),
                                        identb[:, :])
                last.then_inc(filled, 1)

            for task, u in SETUP_TASKS:
                run(task, u)
            pe.wait_ge(consts_made, 2)
            for g in SLOTS:
                for p in range(8):
                    if p % 2 == 0 and g >= 0 and live(g // 2):
                        second_pass(g, p // 2)
                    if p % 2 == 1 and g + 2 in chunk_base:
                        for i, chunk in max_part(g + 2, p):
                            first_pass(g + 2, i, chunk)
                    if p == 2 and g - 1 in half_no:
                        values_pass(g - 1, 1)
                    if p == 6 and g in half_no:
                        values_pass(g, 0)
                    for task, u in bench_tasks(g, p):
                        run(task, u)

        @block.scalar
        def _(act):
            def ready(task, u):
                act.wait_ge(filled, turn(task, u) + 1)

            def run(task, u):
                if task == "lora_turn":
                    ready(task, u)
                    act.activation(lo_bt[:, :, :].rearrange("r a d -> r (a d)"), bench[0:RANK, :], ACT.Copy,
                                   scale=1.0 / RANK).then_inc(cleared, 1)
                elif task == "lora_merge":
                    ready(task, u)
                    act.activation(w[:, 0].rearrange("p a d -> p (a d)"), bench[:, :], ACT.Copy).then_inc(cleared, 1)
                elif task == "max_rows":
                    g = u
                    ready(task, g)
                    if g >= 2 and g - 2 in half_no:
                        act.wait_ge(max_stored, max_store_count(g - 2))
                    if kind(g // 2) == CLASS:
                        act.activation(mtx[:, g % 2, :], bench16[0:6, S:S + P], ACT.Copy)
                    act.activation(mt[:, g % 2, :], bench16[0:3 * HH, 0:S], ACT.Copy).then_inc(cleared, 1)
                elif task == "turn_x":
                    ready(task, u)
                    act.activation(xt[:, u % 2, :], bench[:, 0:S], ACT.Copy).then_inc(cleared, 1)
                elif task == "turn_x3":
                    ready(task, u)
                    act.activation(xt3[:, UNITS[u][1], :], bench[:, 0:S], ACT.Copy).then_inc(cleared, 1)
                elif task == "turn_ctx":
                    ready(task, u)
                    act.activation(cx[:, u % 2, :], bench[:, 0:S], ACT.Copy).then_inc(cleared, 1)
                elif task in ("qk", "qk3"):
                    ready(task, u)
                    i = part_order[u + (B + 2 if task == "qk3" else 0)]
                    act.wait_ge(parts_stored, 16 * i)
                    first = parts[:, 0, :, :].rearrange("p a q -> p (a q)")
                    if task == "qk" and kind(u) == CROSS:
                        act.wait_ge(small_in, 16 * 8)
                        for a in range(2):
                            last = act.activation(parts[:, 0, a, :], bench[:, S * a:S * (a + 1)], ACT.Identity,
                                                  bias=qk_bias[:, a:a + 1])
                    else:
                        last = act.activation(first, bench[:, :], ACT.Copy)
                    last.then_inc(part1_ready, 1)
                    act.wait_ge(cleared, turn(task, u) + 1)
                    act.activation(parts[:, 1, :, :], rest[:, :, :], ACT.Copy).then_inc(part2_ready, 1)
                elif task == "q_tokens":
                    ready(task, u)
                    act.wait_ge(stats3_ready, UNITS[u][1])
                    act.activation(sq[:, :], bench[:, 0:S], ACT.Square).then_inc(sq_ready, 1)
                elif task == "turn_heads":
                    ready(task, u)
                    act.activation(heads_t[:, :], bench[:, 0:S], ACT.Copy).then_inc(cleared, 1)
                elif task == "reg_scores":
                    ready(task, u)
                    act.activation(px[:, :, :, :].rearrange("p h t c -> p (h t c)"), bench[:, 0:HH * NT * XC],
                                   ACT.Exp, scale=SCALE).then_inc(cleared, 1)
                elif task == "reg_values":
                    ready(task, u)
                    act.activation(otx[:, :, :].rearrange("p q c -> p (q c)"), bench[:, 0:2 * XC],
                                   ACT.Copy).then_inc(cleared, 1)
                elif task == "turn_class":
                    ready(task, u)
                    act.activation(cls_t[:, :], bench16[0:4 * B * NT, 0:P], ACT.Copy).then_inc(cleared, 1)

            def exponentials(g, c):
                i = NCHB * half_no[g] + c
                wd = WIDTH[kind(g // 2)]
                act.wait_ge(scores, i + 1)
                if i >= 4:
                    act.wait_ge(pv_done, (i - 4) // 2 + 1)
                act.activation(pr[:, i % 4, :, 0:wd], ps_b[:, i % 2, :, 0:wd], ACT.Exp, scale=SCALE).then_inc(exp_done, 1)

            def copy_out(g):
                act.wait_ge(pv_done, 2 * half_no[g] + 2)
                if half_no[g] >= 2:
                    act.wait_ge(filled, turn("turn_out", live_halves[half_no[g] - 2]) + 1)
                act.activation(ot[:, g % 2, :, :], ps_v[:, :, :], ACT.Copy).then_inc(ot_ready, 1)

            for task, u in SETUP_TASKS:
                run(task, u)
            for g in SLOTS:
                for p in range(8):
                    if p % 2 == 0 and g >= 0 and live(g // 2):
                        exponentials(g, p // 2)
                    if p == 2 and g - 1 in half_no:
                        copy_out(g - 1)
                    for task, u in bench_tasks(g, p):
                        run(task, u)

        @block.vector
        def _(dve):
            steps = [0]

            def link(ins):
                steps[0] += 1
                ins.then_inc(dve_step, 1)
                dve.wait_ge(dve_step, steps[0])

            def take_max(g, i, chunk):
                what, h1 = chunk
                no = chunk_base[g] + i
                dve.wait_ge(max_scores, no + 1)
                bank = ps_a[:, no % 2, :]
                m = nm[:, g % 2]
                if what == "reg":
                    src, dst = bank.rearrange("p (a k) -> p a k", a=2), nx[:, g % 2, :]
                elif what == "tile0":
                    src, dst = bank.rearrange("p (a k) -> p a k", a=4), m[:, 0, h1:h1 + 4]
                elif what == "tile1":
                    src, dst = bank.rearrange("p (a k) -> p a k", a=2), m[:, 1, h1:h1 + 2]
                elif what == "window":
                    src, dst = bank[:, 0:2 * WW].rearrange("p (a k) -> p a k", a=2), m[:, :, h1]
                else:
                    src, dst = bank.rearrange("p (a k) -> p a k", a=2), m[:, :, h1]
                dve.tensor_reduce(dst, src, AX.X, ALU.max, negate=True).then_inc(max_taken, 1)

            def split_max(g):
                m, k = nm[:, g % 2], mp[:, g % 2]
                dve.wait_ge(max_taken, chunk_base[g] + len(max_chunks(g)))
                if half_no[g] >= 2:
                    dve.wait_ge(filled, turn("max_rows", live_halves[half_no[g] - 2]) + 1)
                link(dve.tensor_copy(k[:, :, 0, :], m))
                link(dve.tensor_tensor(nmr[:, :, :], m, k[:, :, 0, :], ALU.subtract))
                link(dve.tensor_copy(k[:, :, 1, :], nmr[:, :, :]))
                last = dve.tensor_tensor(k[:, :, 2, :], nmr[:, :, :], k[:, :, 1, :], ALU.subtract)
                if kind(g // 2) == CLASS:
                    m, k = nx[:, g % 2, :], mpx[:, g % 2]
                    link(last)
                    link(dve.tensor_copy(k[:, 0, :], m))
                    link(dve.tensor_tensor(nxr[:, :], m, k[:, 0, :], ALU.subtract))
                    link(dve.tensor_copy(k[:, 1, :], nxr[:, :]))
                    last = dve.tensor_tensor(k[:, 2, :], nxr[:, :], k[:, 1, :], ALU.subtract)
                last.then_inc(max_parts, 1)

            def norm(what, u):
                i = norm_order[u]
                three = u >= NU
                b = UNITS[u - NU][1] if three else UNITS[u][1]
                if what == "stats":
                    if three:
                        dve.wait_ge(cleared, turn("project", CROSS0 + b) + 1)
                    elif kind(u) == CROSS:
                        dve.wait_ge(cleared, turn("project", b) + 1)
                    elif b == 0:
                        dve.wait_ge(x_first, 16)
                    else:
                        dve.wait_ge(x_rest, 16 * (B - 1))
                    for t in range(NT):
                        link(dve.bn_stats(st6[:, t, :], xr[:, b, t, :]))
                    for t in range(NT):
                        link(dve.bn_aggr(mv[:, t, :], st6[:, t, :]))
                    if i > 0:
                        dve.wait_ge(rstd_ready, i)
                    dve.tensor_scalar(ve[:, :], mv[:, :, 1], EPS, None, ALU.add).then_inc(stats_ready, 1)
                else:
                    dve.wait_ge(rstd_ready, i + 1)
                    if i > 0:
                        before = [k for k in norm_order if norm_order[k] == i - 1][0]
                        task = ("turn_x3", before - NU - B - 2) if before >= NU else ("turn_x", before)
                        dve.wait_ge(filled, turn(*task) + 1)
                    for t in range(NT):
                        last = dve.tensor_scalar(xn[:, t, :], xr[:, b, t, :], mv[:, t, 0:1], rs[:, t:t + 1],
                                                 ALU.subtract, ALU.mult)
                    last.then_inc(xn_ready, 1)

            def ready(task, u):
                dve.wait_ge(filled, turn(task, u) + 1)

            def run(task, u):
                if task in ("qk", "qk3"):
                    i = part_order[u + (B + 2 if task == "qk3" else 0)]
                    dve.wait_ge(part1_ready, i + 1)
                    if task == "qk" and kind(u) == CROSS:
                        for a in range(2):
                            last = dve.scalar_tensor_tensor(rest[:, a, :], bench[:, S * a:S * (a + 1)],
                                                            qk_bias[:, a:a + 1], parts[:, 0, a, :],
                                                            ALU.add, ALU.subtract)
                    else:
                        last = dve.tensor_tensor(rest[:, :, :].rearrange("p a q -> p (a q)"), bench[:, :],
                                                 parts[:, 0, :, :].rearrange("p a q -> p (a q)"), ALU.subtract)
                    last.then_inc(cleared, 1)
                    dve.wait_ge(cleared, turn(task, u) + 1)
                    dve.wait_ge(part2_ready, i + 1)
                    dve.tensor_tensor(parts[:, 2, :, :], rest[:, :, :], parts[:, 1, :, :],
                                      ALU.subtract).then_inc(parts_ready, 1)
                elif task == "q_tokens":
                    b = UNITS[u][1]
                    dve.wait_ge(sq_ready, b + 1)
                    if b == 0:
                        dve.wait_ge(g_pow, 2)
                    for t in range(NT):
                        last = dve.tensor_tensor(dg[:, D * t:D * (t + 1)], bench[:, P * t:P * (t + 1)], g_hat[:, :], ALU.mult)
                    last.then_inc(cleared, 1)
                    dve.wait_ge(cleared, turn(task, u) + 1)
                    link(dve.tensor_reduce(dq[:, b, :], dg[:, :].rearrange("p (h d) -> p h d", d=HD), AX.X, ALU.add))
                    dve.tensor_reduce(n2[:, b, :], sq[:, :].rearrange("p (h d) -> p h d", d=HD), AX.X,
                                      ALU.add).then_inc(stats3_ready, 1)
                elif task == "values":
                    ready(task, u)
                    buf = u % 2
                    prev = unit_no[u] - 2
                    if prev >= 0:
                        dve.wait_ge(pv_done, 4 * (prev + 1))
                    else:
                        dve.wait_ge(stacks_zero, 3)
                    if kind(u - 2) == CLASS:
                        dve.wait_ge(filled, turn("reg_values", 2 * (u - 2) + 1) + 1)
                    dst = vv[:, buf, :, :, 0:HD]
                    src = bench[:, 0:S].rearrange("p (t h d) -> p t h d", t=NT, d=HD)
                    if kind(u) == CROSS:
                        dve.wait_ge(small_in, 16 * 8)
                        for t in range(NT):
                            last = dve.tensor_tensor(dst[:, t], src[:, t],
                                                     v_bias[:, :].rearrange("p (h d) -> p h d", d=HD), ALU.add)
                    else:
                        last = dve.tensor_copy(dst, src)
                    last.then_inc(cleared, 1)
                elif task == "turn_out":
                    g = u
                    ready(task, g)
                    if g % 2 == 0 and live_halves.index(g) >= 2:
                        before = live_halves[half_no[g] - 2] // 2
                        dve.wait_ge(filled, turn("turn_heads", before) + 1)
                    v = bench[:, :].rearrange("p (x c) -> p x c", c=32)
                    h1 = HH * HD * (g % 2)
                    link(dve.reciprocal(rec[:, :], v[:, :, HD]))
                    dst = heads[:, :, h1:h1 + HH * HD].rearrange("p t (x d) -> p t x d", d=HD)
                    src = bench[:, :].rearrange("p (t x c) -> p t x c", t=NT, c=32)[:, :, :, 0:HD]
                    r = rec[:, :].rearrange("p (t x) -> p t x", t=NT).unsqueeze(3).broadcast_to([P, NT, HH, HD])
                    last = dve.tensor_tensor(dst, src, r, ALU.mult)
                    if kind(g // 2) == CLASS:
                        link(last)
                        a = heads[0:REG, 0, h1:h1 + HH * HD]
                        link(dve.tensor_tensor(a, a, hx[0:REG, g % 2, :], ALU.add))
                        last = dve.tensor_scalar(a, a, 0.5, None, ALU.mult)
                    last.then_inc(cleared, 1)
                elif task == "project":
                    ready(task, u)
                    b = UNITS[u][1]
                    if kind(u) != SELF:
                        dve.wait_ge(bias_added, bias_count(u + NU if kind(u) == CLASS else u))
                    dst = xr[:, b].rearrange("p t d -> p (t d)")
                    dve.tensor_tensor(dst, bench[:, 0:S], dst, ALU.add).then_inc(cleared, 1)
                elif task == "reg_turn":
                    g = u
                    ready(task, g)
                    v = bench[0:XC, 0:2 * GV].rearrange("p (x c) -> p x c", c=32)
                    link(dve.reciprocal(recx[:, :], v[:, :, HD]))
                    dve.tensor_tensor(hx[:, g % 2, :].rearrange("p (x d) -> p x d", d=HD), v[:, :, 0:HD],
                                      recx[:, :].unsqueeze(2).broadcast_to([XC, HH, HD]), ALU.mult).then_inc(cleared, 1)

            def classes():
                dve.wait_ge(rn_ready, B)
                link(dve.tensor_tensor(sh[:, :, :], dq[:, :, :], rn[:, :, :], ALU.mult))
                link(dve.tensor_reduce(sim[:, 2], sh[:, :, :].rearrange("p b (t h) -> p b t h", h=NH), AX.X, ALU.add))
                link(dve.tensor_scalar(sim[:, 0], sim[:, 2], 1.0 / NH, None, ALU.mult))
                link(dve.tensor_copy(sim[:, 1], sim[:, 0]))
                link(dve.tensor_scalar(sim[:, 2], sim[:, 0], -1.0, None, ALU.mult))
                link(dve.memset(sim[0:REG, 1:3, :, 0], -3.0e38))
                link(dve.tensor_reduce(ends[:, 0:1], sim[:, 1], AX.XY, ALU.max))
                dve.tensor_reduce(ends[:, 1:2], sim[:, 2], AX.XY, ALU.max).then_inc(ends_ready, 1)
                dve.wait_ge(ends_done, 1)
                link(dve.tensor_tensor(span[:, 0:1], ends_all[:, 0:1], ends_all[:, 1:2], ALU.add))
                link(dve.reciprocal(span[:, 1:2], span[:, 0:1]))
                link(dve.tensor_scalar(sim[:, 1], sim[:, 0], ends_all[:, 1:2], span[:, 1:2], ALU.add, ALU.mult))
                link(dve.tensor_scalar(pos[:, :, :], sim[:, 1], SIM_CUT, None, ALU.is_gt))
                link(dve.tensor_copy(cls[:, 0], pos[:, :, :]))
                link(dve.tensor_scalar(cls[:, 1], pos[:, :, :], -1.0, 1.0, ALU.mult, ALU.add))
                link(dve.tensor_scalar(cls[:, 2], pos[:, :, :], -MASKED, MASKED, ALU.mult, ALU.add))
                link(dve.tensor_scalar(cls[:, 3], pos[:, :, :], MASKED, None, ALU.mult))
                link(dve.memset(cls[0:REG, 0, :, 0], 0.0))
                link(dve.memset(cls[0:REG, 1, :, 0], 1.0))
                dve.memset(cls[0:REG, 2:4, :, 0], 0.0).then_inc(cls_ready, 1)

            dve.memset(ks[:, 0].rearrange("p h q -> p (h q)").bitcast(F32), 0.0).then_inc(dve_step, 1)
            dve.memset(ks[:, 1].rearrange("p h q -> p (h q)").bitcast(F32), 0.0).then_inc(dve_step, 1)
            steps[0] = 2
            dve.wait_ge(dve_step, 2)
            link(dve.memset(ks[MROW:P], 1.0))
            dve.memset(qs[:, 1].rearrange("p h q -> p (h q)").bitcast(F32), 0.0).then_inc(stacks_zero, 1)
            for g in SLOTS:
                for p in range(8):
                    if p % 2 == 1 and g + 2 in chunk_base:
                        for i, chunk in max_part(g + 2, p):
                            take_max(g + 2, i, chunk)
                        if p == 7 and g + 2 in half_no:
                            split_max(g + 2)
                    for task, u in bench_tasks(g, p):
                        if task == "turn_class":
                            continue
                        run(task, u)
                    for what, u in norm_tasks(g, p):
                        norm(what, u)
                    if g == 2 * (CLASS0 - 2) + 1 and p == 3:
                        classes()

        @block.gpsimd
        def _(pool):
            steps = [0]

            def link(ins):
                steps[0] += 1
                ins.then_inc(pool_step, 1)
                pool.wait_ge(pool_step, steps[0])

            def mask(g, c):
                i = NCHB * half_no[g] + c
                k = kind(g // 2)
                pool.wait_ge(exp_done, i + 1)
                p = pr[:, i % 4]
                if k == SELF:
                    both = p.rearrange("p h (a q) -> p h a q", q=S)[:, :, :, 0:P]
                    pool.affine_select(out=both, in_=both, compare_op=ALU.is_ge, fill=0.0, base=0,
                                       pattern=[[0, 2], [0, 2], [1, P]], channel_multiplier=-1).then_inc(masked, 1)
                else:
                    for at, m, base, s in ((0, WIN, WIN, 1), (WIN, P, 0, -1), (WW, P, 0, 1), (WW + P, WIN, 0, -1)):
                        v = p[:, :, at:at + m]
                        last = pool.affine_select(out=v, in_=v, compare_op=ALU.is_ge, fill=0.0, base=base,
                                                  pattern=[[0, 2], [s, m]], channel_multiplier=-s)
                    last.then_inc(masked, 1)

            link(pool.memset(ident[:, :], 0.0))
            pool.affine_select(out=ident[:, :], in_=ident[:, :], compare_op=ALU.not_equal, fill=1.0, base=0,
                               pattern=[[-1, P]], channel_multiplier=1).then_inc(ident_made, 1)
            link(pool.memset(identb[:, :], 0.0))
            pool.affine_select(out=identb[:, :], in_=identb[:, :], compare_op=ALU.not_equal, fill=1.0, base=0,
                               pattern=[[-1, P]], channel_multiplier=1).then_inc(ident_made, 1)
            link(pool.memset(neg_half[:, :], -0.5))
            link(pool.memset(mask_c[:, :, :], 0.0))
            link(pool.memset(mask_w[:, :, :], 0.0))
            pool.affine_select(out=mask_c[:, :, :], in_=mask_c[:, :, :], compare_op=ALU.is_ge, fill=MASKED, base=0,
                               pattern=[[0, 4], [-1, P]], channel_multiplier=1).then_inc(consts_made, 1)
            for t, b1, b2 in ((0, WIN, WIN), (1, 2 * WIN, 0)):
                v = mask_w[:, t, :]
                link(pool.affine_select(out=v, in_=v, compare_op=ALU.is_ge, fill=MASKED, base=b1,
                                        pattern=[[-1, WW]], channel_multiplier=1))
                last = pool.affine_select(out=v, in_=v, compare_op=ALU.is_ge, fill=MASKED, base=b2,
                                          pattern=[[1, WW]], channel_multiplier=-1)
            last.then_inc(consts_made, 1)
            pool.memset(qs[:, 0].rearrange("p h q -> p (h q)").bitcast(F32), 0.0).then_inc(stacks_zero, 1)
            link(pool.memset(vv[:, :, :, :, :], 0.0))
            pool.memset(vv[:, :, :, :, HD:HD + 1], 1.0).then_inc(stacks_zero, 1)
            pool.memset(qx[:, :, :, :], 0.0).then_inc(qx_made, 1)
            link(pool.memset(qx_cls[:, :, :, :, :], 0.0))
            pool.memset(qx_cls[:, 0, :, :, 0:REG], 1.0).then_inc(qx_made, 1)

            def reciprocal_deviation(i):
                pool.wait_ge(stats_ready, i + 1)
                if i > 0:
                    pool.wait_ge(xn_ready, i)
                pool.tensor_tensor(rs[:, :], ve[:, :], neg_half[:, 0:NT], ALU.pow).then_inc(rstd_ready, 1)

            for g in SLOTS:
                n, h = g // 2, g % 2
                for p in range(8):
                    if p % 2 == 0 and g >= 0 and kind(g // 2) in (SELF, CROSS):
                        mask(g, p // 2)
                    for what, u in norm_tasks(g, p):
                        i = norm_order[u]
                        if what == "stats":
                            reciprocal_deviation(i)
                        elif u >= NU or kind(u) == CROSS:
                            three = u >= NU
                            b = UNITS[u - NU][1] if three else UNITS[u][1]
                            pool.wait_ge(xn_ready, i + 1)
                            pool.wait_ge(small_in, 16 * 8)
                            for t in range(NT):
                                v = xr[:, b, t, :]
                                last = pool.tensor_tensor(v, v, o_bias[:, 1 if three else 0, :], ALU.add)
                            last.then_inc(bias_added, 1)
                    if p == 5 and h == 1 and kind(n - 1) == CROSS:
                        b = UNITS[n - 1][1]
                        pool.wait_ge(stats3_ready, b + 1)
                        pool.tensor_tensor(rn[:, b, :], n2[:, b, :], neg_half[:, :], ALU.pow).then_inc(rn_ready, 1)
                    if p == 0 and g + 2 in half_no and kind((g + 2) // 2) == CLASS:
                        gg = g + 2
                        buf, h0 = (gg // 2) % 2, HH * (gg % 2)
                        pool.wait_ge(stack_sem(gg), stack_count(gg))
                        if gg - 4 in half_no and kind((gg - 4) // 2) == CLASS:
                            pool.wait_ge(filled, turn("reg_scores", gg - 4) + 1)
                        pool.tensor_copy(qx[0:CLS, buf, h0:h0 + HH, 0:REG],
                                         qs[0:CLS, buf, h0:h0 + HH, 0:REG]).then_inc(qx_ready, 1)
                if g == 0:
                    pool.wait_ge(small_in, 16 * 8)
                    link(pool.tensor_tensor(g_sq[:, :], g_row[:, :], g_row[:, :], ALU.mult))
                    v = g_sq[:, :].rearrange("p (h d) -> p h d", d=HD)
                    link(pool.tensor_tensor(v[:, :, 0:4], v[:, :, 0:4], v[:, :, 4:8], ALU.add))
                    link(pool.tensor_tensor(v[:, :, 0:2], v[:, :, 0:2], v[:, :, 2:4], ALU.add))
                    link(pool.tensor_tensor(g_n2[:, :], v[:, :, 0], v[:, :, 1], ALU.add))
                    pool.tensor_tensor(g_rn[:, :], g_n2[:, :], neg_half[:, 0:NH], ALU.pow).then_inc(g_pow, 1)
                    pool.wait_ge(g_pow, 1)
                    pool.tensor_tensor(g_hat[:, :].rearrange("p (h d) -> p h d", d=HD),
                                       g_row[:, :].rearrange("p (h d) -> p h d", d=HD),
                                       g_rn[:, :].unsqueeze(2).broadcast_to([P, NH, HD]), ALU.mult).then_inc(g_pow, 1)
                if g == 2 * (CLASS0 - 2) + 1:
                    pool.wait_ge(ends_ready, 1)
                    pool.partition_all_reduce(ends_all[:, :], ends[:, :], P, RMAX).then_inc(ends_done, 1)


_INS = ['x', 'ctx_1024', 'L0_attn_wq', 'L0_attn_aq', 'L0_attn_bq', 'L0_attn_wk', 'L0_attn_ak', 'L0_attn_bk',
        'L0_attn_wv', 'L0_attn_av', 'L0_attn_bv', 'L0_attn_wo', 'L0_attn_ao', 'L0_attn_bo', 'L0_xattn_Wq',
        'L0_xattn_bq', 'L0_xattn_Wk', 'L0_xattn_bk', 'L0_xattn_Wv', 'L0_xattn_bv', 'L0_xattn_Wo', 'L0_xattn_bo',
        'L0_ffn_g_info', 'L0_ffn_W_qkv', 'L0_ffn_W_proj', 'L0_ffn_b_proj']
_OUTS = [((8, 256, 128), 'float32')]


def kernel(**inputs):
    import numpy as _np
    import concourse.bacc as _bacc
    from concourse import mybir as _mybir
    from concourse.bass_utils import run_bass_kernel_spmd as _run

    nc = _bacc.Bacc("TRN2", target_bir_lowering=False, num_devices=1)
    arrays, args = {}, []
    for name in _INS:
        a = _np.ascontiguousarray(inputs[name])
        arrays[f"in_{name}_dram"] = a
        args.append(nc.dram_tensor(f"in_{name}_dram", a.shape, _mybir.dt.from_np(a.dtype), kind="ExternalInput").ap())
    for i, (shape, dtype) in enumerate(_OUTS):
        dt = _mybir.dt.from_np(_np.dtype(dtype))
        args.append(nc.dram_tensor(f"out_{i}_dram", shape, dt, kind="ExternalOutput").ap())
    layer_kernel(nc, *args)
    r = _run(nc, [arrays], core_ids=[0])
    got = tuple(r.results[0][f"out_{i}_dram"] for i in range(len(_OUTS)))
    return got[0]
```

```python
from contextlib import ExitStack

import concourse.bass as bass
from concourse import mybir

F32 = mybir.dt.float32
BF16 = mybir.dt.bfloat16
ALU = mybir.AluOpType
ACT = mybir.ActivationFunctionType
AX = mybir.AxisListType
RMAX = bass.bass_isa.ReduceOp.max

SELF, CROSS, CLASS, IDLE = "self", "cross", "class", "idle"
Q, K, V_, O = range(4)
MASKED = -1.0e30
EPS = 1e-5
SIM_CUT = 0.9
REG = 5

TERMS = [(0, 2), (0, 1), (0, 0), (1, 0), (2, 0), (1, 1)]


def layer_kernel(nc: bass.Bass, x, ctx_1024, L0_attn_wq, L0_attn_aq, L0_attn_bq, L0_attn_wk, L0_attn_ak,
                 L0_attn_bk, L0_attn_wv, L0_attn_av, L0_attn_bv, L0_attn_wo, L0_attn_ao, L0_attn_bo,
                 L0_xattn_Wq, L0_xattn_bq, L0_xattn_Wk, L0_xattn_bk, L0_xattn_Wv, L0_xattn_bv, L0_xattn_Wo,
                 L0_xattn_bo, L0_ffn_g_info, L0_ffn_W_qkv, L0_ffn_W_proj, L0_ffn_b_proj, out):
    B, S, D = x.shape
    RANK = L0_attn_aq.shape[0]
    NH = 16
    HD = D // NH
    P = 128
    NT = S // P
    HH = NH // 2
    WIN = 64
    WW = P + WIN
    NTERM = len(TERMS)
    CLS = HD * NTERM
    MROW = 96
    KA = MROW
    KB = MROW + 3
    RING = 12
    NSTORE = 16 * 6
    SCALE = float(HD) ** -0.5
    GV = 4 * 32
    XC = 8
    assert D == P and S == 2 * P and HD == 8

    UNITS = ([(SELF, b) for b in range(B)] + [(CROSS, b) for b in range(B)] + [(IDLE, 0)] * 2
             + [(CLASS, b) for b in range(B)])
    CROSS0, CLASS0, NU = B, 2 * B + 2, len(UNITS)

    def kind(u):
        return UNITS[u][0] if 0 <= u < NU else IDLE

    def live(u):
        return kind(u) != IDLE

    STG = {SELF: 0, CROSS: 1, CLASS: 2}

    AT0 = dict(max_rows=0, turn_x=1, turn_ctx=1, qk=3, part2=5, part3=5, turn_out=4, turn_heads=6,
               project=7, reg_scores=4, reg_turn=2, reg_values=6, stats3=7, copy_out=0, values_b=0,
               values_a=7)
    AT1 = dict(max_rows=0, turn_x3=2, qk3=5, part2=6, part3=6, q_tokens=5, turn_out=7, values=6,
               reg_scores=5, reg_turn=3, reg_values=7, scale3=0, stats=4, scale=7, copy_out=4, values_b=0,
               values_a=7)

    def bench_tasks(g, p):
        n, h = g // 2, g % 2
        at = (AT0, AT1)[h]
        t = []
        if p == at["max_rows"] and live((g + 1) // 2):
            t.append(("max_rows", g + 1))
        if p == at["reg_scores"] and kind(n) == CLASS:
            t.append(("reg_scores", g))
        if p == at["reg_values"] and kind(n) == CLASS:
            t.append(("reg_values", g))
        if p == at["reg_turn"] and kind((g - 1) // 2) == CLASS:
            t.append(("reg_turn", g - 1))
        if h == 0:
            u = n + 2
            if p == at["turn_x"] and kind(u) in (SELF, CROSS):
                t.append(("turn_x", u))
            if p == at["turn_ctx"] and u == CROSS0:
                t.append(("turn_bias", 0))
            if p == at["turn_ctx"] and kind(u) == CROSS:
                t.append(("turn_ctx", u))
            if p == at["qk"] and kind(u) in (SELF, CROSS):
                t.append(("qk", u))
            if p == at["turn_out"] and live(n - 1):
                t.append(("turn_out", g - 1))
            if p == at["turn_heads"] and live(n - 1):
                t.append(("turn_heads", n - 1))
            if p == at["project"] and live(n - 1):
                t.append(("project", n - 1))
        else:
            if p == at["turn_x3"] and kind(n - 1) == CROSS:
                t.append(("turn_x3", n - 1))
            if p == at["qk3"] and kind(n - 1) == CROSS:
                t.append(("qk3", n - 1))
            if p == at["q_tokens"] and kind(n - 1) == CROSS:
                t.append(("q_tokens", n - 1))
            if p == at["turn_out"] and live(n):
                t.append(("turn_out", g - 1))
            if p == at["values"] and live(n + 1):
                t.append(("values", n + 1))
            if p == 7 and n == CLASS0 - 2:
                t.append(("turn_class", 0))
        return t

    def part_tasks(g, p):
        n, h = g // 2, g % 2
        at = (AT0, AT1)[h]
        u = n + 2 if h == 0 and kind(n + 2) in (SELF, CROSS) else n - 1 + B + 2 if h == 1 and kind(n - 1) == CROSS else None
        return [(what, u) for what in ("part2", "part3") if u is not None and p == at[what]]

    FIRST, LAST = -5, 2 * NU + 2
    SLOTS = range(FIRST, LAST)
    SETUP_TASKS = [("lora_turn", 0), ("lora_merge", 0)]
    bench_order, norm_order, part_order = {}, {}, {}
    for task in SETUP_TASKS:
        bench_order[task] = len(bench_order)
    for g in SLOTS:
        for p in range(8):
            for task in bench_tasks(g, p):
                bench_order[task] = len(bench_order)

    def norm_tasks(g, p):
        n, h = g // 2, g % 2
        t = []
        if h == 1 and kind(n - 1) == CROSS and p == AT1["scale3"]:
            t.append(("scale", n - 1 + B + 2 + NU))
        if h == 0 and kind(n - 1) == CROSS and p == AT0["stats3"]:
            t.append(("stats", n - 1 + B + 2 + NU))
        if h == 1 and kind(n + 3) in (SELF, CROSS):
            if p == AT1["stats"]:
                t.append(("stats", n + 3))
            if p == AT1["scale"]:
                t.append(("scale", n + 3))
        return t

    for g in SLOTS:
        for p in range(8):
            for what, u in norm_tasks(g, p):
                if what == "stats":
                    norm_order[u] = len(norm_order)
            for what, u in bench_tasks(g, p):
                if what in ("qk", "qk3"):
                    part_order[u + (B + 2 if what == "qk3" else 0)] = len(part_order)

    def turn(task, u):
        return bench_order[(task, u)]

    def max_chunks(g):
        if g < 0:
            return []
        k = kind(g // 2)
        if k == SELF:
            return ([("tile0", 4 * i) for i in range(HH // 4)] + [("tile1", 2 * i) for i in range(HH // 2)])
        if k == CROSS:
            return [("window", i) for i in range(HH)]
        if k == CLASS:
            return [("full", i) for i in range(HH)] + [("reg", 0)]
        return []

    chunk_base = {}
    total = 0
    for g in range(0, 2 * NU):
        chunk_base[g] = total
        total += len(max_chunks(g))

    def max_part(g, p):
        c = max_chunks(g)
        lo, hi = len(c) * p // 8, len(c) * (p + 1) // 8
        return [(i, c[i]) for i in range(lo, hi)]

    live_halves = [g for g in range(2 * NU) if live(g // 2)]
    half_no = {g: i for i, g in enumerate(live_halves)}
    unit_no = {u: half_no[2 * u] // 2 for u in range(NU) if live(u)}
    SPANS = {SELF: ((0, 0, S), (1, P, S)), CROSS: ((0, 0, WW), (1, S - WW, S)), CLASS: ((0, 0, S), (1, 0, S))}
    WIDTH = {SELF: S + P, CROSS: 2 * WW, CLASS: 2 * S}

    with ExitStack() as ctx:
        def sb(name, shape, dt=F32):
            return ctx.enter_context(nc.sbuf_tensor(name, shape, dt))

        def sem(name):
            return ctx.enter_context(nc.semaphore(name))

        xr = sb("xr", [P, B, NT, D])
        ct = sb("ct", [P, B, NT, D])
        w = sb("w", [P, 3, 4, D])
        w_dh = sb("w_dh", [P, 3, 2, D])
        row_dh = sb("row_dh", [1, 2, D])
        wraw = sb("wraw", [P, 4, D])
        lo_a = sb("lo_a", [RANK, 4, D])
        lo_b = sb("lo_b", [P, 4, RANK])
        lo_bt = sb("lo_bt", [RANK, 4, D])
        qk_row = sb("qk_row", [1, 2, D])
        qk_bias = sb("qk_bias", [P, 2])
        v_bias = sb("v_bias", [P, D])
        o_bias = sb("o_bias", [P, 2, D])
        g_row = sb("g_row", [P, D])
        g_sq = sb("g_sq", [P, D])
        g_n2 = sb("g_n2", [P, NH])
        g_rn = sb("g_rn", [P, NH])
        g_hat = sb("g_hat", [P, D])
        ident = sb("ident", [P, P])
        identb = sb("identb", [P, P], BF16)
        mask_c = sb("mask_c", [P, 4, P], BF16)
        mask_w = sb("mask_w", [P, NT, WW], BF16)
        neg_half = sb("neg_half", [P, NT * NH])
        stk = sb("stk", [P, 2, NH, 2, S], BF16)
        qx = sb("qx", [P, 2, NH, 32], BF16)
        qx_cls = sb("qx_cls", [1, 2, 2, NH, 32], BF16)
        pr = sb("pr", [P, RING, 2 * S])
        vv = sb("vv", [P, 2, NT, NH, 32])
        ot = sb("ot", [P, 2, 2, S])
        heads = sb("heads", [P, NT, D])
        heads_t = sb("heads_t", [P, S])
        rec = sb("rec", [P, NT * HH])
        st6 = sb("st6", [P, NT, 6])
        mv = sb("mv", [P, NT, 2])
        ve = sb("ve", [P, NT])
        rs = sb("rs", [P, NT])
        xn = sb("xn", [P, NT, D])
        xt = sb("xt", [P, 2, S])
        cx = sb("cx", [P, 2, S])
        xt3 = sb("xt3", [P, B, S])
        rest = sb("rest", [P, 2, S])
        parts = sb("parts", [P, 3, 2, S], BF16)
        nm = sb("nm", [P, 2, NT, HH])
        nmr = sb("nmr", [P, NT, HH])
        mp = sb("mp", [P, 2, NT, 3, HH], BF16)
        mt = sb("mt", [3 * HH, 2, S], BF16)
        nx = sb("nx", [P, 2, 2])
        nxr = sb("nxr", [P, 2])
        mpx = sb("mpx", [P, 2, 3, 2], BF16)
        mtx = sb("mtx", [6, 2, P], BF16)
        px = sb("px", [P, HH, NT, XC])
        otx = sb("otx", [P, 2, XC])
        recx = sb("recx", [XC, HH])
        hx = sb("hx", [XC, 2, HH * HD])
        sq = sb("sq", [P, NT * D])
        dg = sb("dg", [P, NT * D])
        n2 = sb("n2", [P, B, NT * NH])
        dq = sb("dq", [P, B, NT * NH])
        rt = sb("rt", [P, B, NT * NH])
        rn = sb("rn", [P, B, NT * NH])
        sh = sb("sh", [P, B, NT * NH])
        sim = sb("sim", [P, 3, B, NT])
        ends = sb("ends", [P, 2])
        ends_all = sb("ends_all", [P, 2])
        span = sb("span", [P, 2])
        pos = sb("pos", [P, B, NT])
        cls = sb("cls", [P, 4, B, NT], BF16)
        cls_t = sb("cls_t", [4 * B * NT, P], BF16)

        ps_a = ctx.enter_context(nc.psum_tensor("ps_a", [P, 2, 512], F32))
        ps_b = ctx.enter_context(nc.psum_tensor("ps_b", [P, 3, 512], F32))
        ps_v = ctx.enter_context(nc.psum_tensor("ps_v", [P, 2, S], F32))
        bench_ps = ctx.enter_context(nc.psum_tensor("bench", [P, 2, 512], F32))

        part_scr = nc.dram_tensor("part_scr", (NU, NTERM, P, 2, S), BF16).ap()
        max_scr = nc.dram_tensor("max_scr", (2 * NU, 3 * HH, S), BF16).ap()
        maxx_scr = nc.dram_tensor("maxx_scr", (2 * NU, 6, P), BF16).ap()
        cls_scr = nc.dram_tensor("cls_scr", (4, B * NT, P), BF16).ap()

        x_first, x_rest, ctx_in, w_lora, w_in, small_in = map(
            sem, ["x_first", "x_rest", "ctx_in", "w_lora", "w_in", "small_in"])
        ident_made, consts_made, stacks_zero, qx_made, g_pow = map(
            sem, ["ident_made", "consts_made", "stacks_zero", "qx_made", "g_pow"])
        dh_ready, vv_zero = sem("dh_ready"), sem("vv_zero")
        pool_step, dve_step = sem("pool_step"), sem("dve_step")
        filled = sem("filled")
        cleared = [sem("cleared0"), sem("cleared1")]
        stats_ready, rstd_ready, xn_ready = map(sem, ["stats_ready", "rstd_ready", "xn_ready"])
        bias_added = sem("bias_added")
        part1_ready, part2_ready, parts_ready = map(sem, ["part1_ready", "part2_ready", "parts_ready"])
        parts_stored = sem("parts_stored")
        stack_ready = [sem(f"stack_ready{i}") for i in range(4)]
        qx_ready = sem("qx_ready")
        max_scores, max_taken, max_parts = map(sem, ["max_scores", "max_taken", "max_parts"])
        max_stored = sem("max_stored")
        max_ready = [sem("max_ready0"), sem("max_ready1")]
        scores, exp_done, masked = map(sem, ["scores", "exp_done", "masked"])
        pv_done, ot_ready = sem("pv_done"), sem("ot_ready")
        sq_ready, stats3_ready, rn_ready = map(sem, ["sq_ready", "stats3_ready", "rn_ready"])
        ends_ready, ends_done, cls_ready, cls_stored = map(
            sem, ["ends_ready", "ends_done", "cls_ready", "cls_stored"])
        stored = sem("stored")

        def bank_of(task, u):
            return bench_ps[:, turn(task, u) % 2, :]

        def wait_cleared(eng, task, u):
            k = turn(task, u)
            eng.wait_ge(cleared[k % 2], k // 2 + 1)

        def part_task(u):
            return ("qk3", u - B - 2) if kind(u) == CLASS else ("qk", u)

        def stack_sem(g):
            return stack_ready[g % 4]

        def stack_count(g):
            total = 0
            for gg in range(g % 4, g + 1, 4):
                if live(gg // 2):
                    total += 16 * (1 + (2 if kind(gg // 2) == CLASS else 0))
            return total

        def max_count(g):
            total = 0
            for gg in range(g % 2, g + 1, 2):
                if live(gg // 2):
                    total += 16 * (2 if kind(gg // 2) == CLASS else 1)
            return total

        CLASS_HALVES = [g for g in live_halves if kind(g // 2) == CLASS]
        def class_no(g):
            return CLASS_HALVES.index(g)

        def max_store_count(g):
            return 16 * sum(2 if kind(gg // 2) == CLASS else 1 for gg in live_halves if gg <= g)

        def bias_count(u):
            return sum(1 for v, i in norm_order.items() if i <= norm_order[u] and (v >= NU or kind(v) == CROSS))

        block = ctx.enter_context(nc.Block())

        @block.sync
        def _(sp):
            def rows(v):
                return v.rearrange("(a n) -> a n", a=1)

            sp.dma_start(xr[:, 0], x[0].rearrange("(t p) d -> p t d", p=P)).then_inc(x_first, 16)
            for i, a in enumerate((L0_attn_wq, L0_attn_wk, L0_attn_wv, L0_attn_wo)):
                sp.dma_start(wraw[:, i, :], a).then_inc(w_lora, 16)
            for i, a in enumerate((L0_attn_aq, L0_attn_ak, L0_attn_av, L0_attn_ao)):
                sp.dma_start(lo_a[:, i, :], a).then_inc(w_lora, 16)
            for i, a in enumerate((L0_attn_bq, L0_attn_bk, L0_attn_bv, L0_attn_bo)):
                sp.dma_start(lo_b[:, i, :], a).then_inc(w_lora, 16)
            sp.dma_start(xr[:, 1:B].rearrange("p b t d -> p (b t) d"),
                         x[1:B].rearrange("b (t p) d -> p (b t) d", p=P)).then_inc(x_rest, 16)

            def stacks(g):
                u, h0, buf = g // 2, HH * (g % 2), (g // 2) % 2
                sp.wait_ge(parts_stored, NSTORE * (part_order[u] + 1))
                if g - 4 >= 0 and live((g - 4) // 2):
                    sp.wait_ge(scores, HH * (half_no[g - 4] + 1))
                if g < 4:
                    sp.wait_ge(stacks_zero, g // 2 + 1)
                sp.dma_start(stk[0:CLS, buf, h0:h0 + HH],
                             part_scr[u].rearrange("t (d h) s q -> (t d) h s q", d=HD)[:, h0:h0 + HH]
                             ).then_inc(stack_sem(g), 16)
                if kind(u) == CLASS:
                    sp.wait_ge(cls_stored, 16)
                    if g - 4 >= 0 and kind((g - 4) // 2) == CLASS:
                        sp.wait_ge(filled, turn("reg_scores", g - 4) + 1)
                    bb = UNITS[u][1]
                    for s in range(2):
                        c = cls_scr[2 * s:2 * s + 2, NT * bb:NT * bb + NT, :].rearrange("k t q -> k (t q)")
                        c = c.unsqueeze(1).broadcast_to([2, HH, S])
                        sp.dma_start(stk[CLS:CLS + 2, buf, h0:h0 + HH, s, :], c).then_inc(stack_sem(g), 16)

            def max_rows(g):
                u, h0, buf = g // 2, HH * (g % 2), (g // 2) % 2
                wait_cleared(sp, "max_rows", g)
                sp.dma_start(max_scr[g], mt[:, g % 2, :]).then_inc(max_stored, 16)
                if kind(u) == CLASS:
                    sp.dma_start(maxx_scr[g], mtx[:, g % 2, :]).then_inc(max_stored, 16)
                sp.wait_ge(max_stored, max_store_count(g))
                sp.dma_start(stk[MROW:MROW + 3, buf, h0:h0 + HH, 0, :],
                             max_scr[g].rearrange("(k h) q -> k h q", k=3)).then_inc(max_ready[g % 2], 16)
                if kind(u) == CLASS:
                    c = maxx_scr[g].rearrange("(k g) c -> k (g c)", k=3).rearrange("k (h r) -> k h r", h=HH)
                    sp.dma_start(qx[MROW:MROW + 3, buf, h0:h0 + HH, :], c).then_inc(max_ready[g % 2], 16)

            def store_parts(u):
                sp.wait_ge(parts_ready, part_order[u] + 1)
                for a in range(3):
                    for s in range(2):
                        at = [t for t in range(NTERM) if TERMS[t][s] == a]
                        step = at[1] - at[0] if len(at) > 1 else 1
                        dst = part_scr[u, at[0]:at[-1] + 1:step, :, s, :].rearrange("t r q -> r t q")
                        src = parts[:, a, s, :].unsqueeze(1).broadcast_to([P, len(at), S])
                        sp.dma_start(dst, src).then_inc(parts_stored, 16)

            def finish(b):
                wait_cleared(sp, "project", CLASS0 + b)
                sp.dma_start(out[b].rearrange("(t p) d -> p t d", p=P), xr[:, b]).then_inc(stored, 16)

            sent_rest = False
            for g in SLOTS:
                n, h = g // 2, g % 2
                if g == 1:
                    sp.dma_start(ct[:, :, :, :].rearrange("p b t d -> p (b t) d"),
                                 ctx_1024.rearrange("b (t p) d -> p (b t) d", p=P)).then_inc(ctx_in, 16)
                    for i, a in enumerate((L0_xattn_Wq, L0_xattn_Wk, L0_xattn_Wv, L0_xattn_Wo)):
                        sp.dma_start(w[:, 1, i, :], a).then_inc(w_in, 16)
                    sp.dma_start(w[:, 2, 0:3, :], L0_ffn_W_qkv.rearrange("i (a o) -> i a o", a=3)).then_inc(w_in, 16)
                    sp.dma_start(w[:, 2, 3, :], L0_ffn_W_proj).then_inc(w_in, 16)
                    for i, a in enumerate((L0_xattn_bq, L0_xattn_bk)):
                        sp.dma_start(qk_row[0:1, i, :], rows(a)).then_inc(small_in, 16)
                    for dst, a in ((v_bias[:, :], rows(L0_xattn_bv)), (o_bias[:, 0, :], rows(L0_xattn_bo)),
                                   (o_bias[:, 1, :], rows(L0_ffn_b_proj)),
                                   (g_row[:, :], L0_ffn_g_info[0, 0:1, :])):
                        sp.dma_start(dst, a.broadcast_to([P, D])).then_inc(small_in, 16)
                    sp.wait_ge(qx_made, 2)
                    for k in range(2):
                        sp.dma_start(qx[CLS + k:CLS + k + 1], qx_cls[0:1, k]).then_inc(small_in, 16)
                if 0 <= g + 3 and live((g + 3) // 2) and kind((g + 3) // 2) != CLASS:
                    stacks(g + 3)
                if live((g + 1) // 2):
                    max_rows(g + 1)
                if n == CLASS0 - 2 and h == 1:
                    wait_cleared(sp, "turn_class", 0)
                    sp.dma_start(cls_scr.rearrange("k t q -> (k t) q"), cls_t[:, :]).then_inc(cls_stored, 16)
                    stacks(2 * CLASS0)
                    stacks(2 * CLASS0 + 1)
                elif kind((g + 3) // 2) == CLASS and g + 3 > 2 * CLASS0 + 1:
                    stacks(g + 3)
                if h == 0 and kind(n + 2) in (SELF, CROSS):
                    store_parts(n + 2)
                if h == 1 and kind(n - 1) == CROSS:
                    store_parts(n - 1 + B + 2)
                if h == 1 and kind(n - 1) == CLASS:
                    finish(UNITS[n - 1][1])
            sp.wait_ge(stored, 16 * B)
            sp.wait_ge(parts_stored, NSTORE * 3 * B)
            sp.wait_ge(max_stored, max_store_count(2 * NU))

        @block.tensor
        def _(pe):
            def begin(task, u):
                k = turn(task, u)
                if k >= 2:
                    pe.wait_ge(cleared[k % 2], k // 2)

            def second_pass(g, c):
                u, buf, h = g // 2, (g // 2) % 2, HH * (g % 2) + c
                i = HH * half_no[g] + c
                if c == 0:
                    pe.wait_ge(max_ready[g % 2], max_count(g))
                if i >= 3:
                    pe.wait_ge(exp_done, i - 2)
                at = 0
                for t, a, b in SPANS[kind(u)]:
                    last = pe.matmul(ps_b[:, i % 3, at:at + b - a], stk[0:KB, buf, h, 1, t * P:(t + 1) * P],
                                     stk[0:KB, buf, h, 0, a:b], start=True, stop=True)
                    at += b - a
                last.then_inc(scores, 1)

            def first_pass(g, i, chunk):
                what, h1 = chunk
                u, buf, h0 = g // 2, (g // 2) % 2, HH * (g % 2)
                no = chunk_base[g] + i
                if i == 0:
                    pe.wait_ge(stack_sem(g), stack_count(g))
                if what == "reg":
                    pe.wait_ge(qx_ready, class_no(g) + 1)
                if no >= 2:
                    pe.wait_ge(max_taken, no - 1)
                bank = ps_a[:, no % 2, :]

                def part(dst, h, t, a, b, start):
                    return pe.matmul(dst, stk[0:KA, buf, h, 0, t * P:(t + 1) * P], stk[0:KA, buf, h, 1, a:b],
                                     start=start, stop=True, skip_group_check=True)

                if what == "tile0":
                    pe.matmul(bank, identb[:, :], mask_c[:, :, :].rearrange("p a b -> p (a b)"),
                              start=True, stop=False, skip_group_check=True)
                    for j in range(4):
                        last = part(bank[:, P * j:P * (j + 1)], h0 + h1 + j, 0, 0, P, False)
                elif what == "tile1":
                    pe.matmul(bank.rearrange("p (a b) -> p a b", a=2)[:, :, P:S], identb[:, :], mask_c[:, 0:2, :],
                              start=True, stop=False, skip_group_check=True)
                    for j in range(2):
                        last = part(bank[:, S * j:S * (j + 1)], h0 + h1 + j, 1, 0, S, False)
                elif what == "window":
                    pe.matmul(bank[:, 0:2 * WW], identb[:, :], mask_w[:, :, :].rearrange("p a b -> p (a b)"),
                              start=True, stop=False, skip_group_check=True)
                    for t in range(NT):
                        a = t * (S - WW)
                        last = part(bank[:, WW * t:WW * (t + 1)], h0 + h1, t, a, a + WW, False)
                elif what == "full":
                    for t in range(NT):
                        last = part(bank[:, S * t:S * (t + 1)], h0 + h1, t, 0, S, True)
                else:
                    for j in range(4):
                        for q in range(2):
                            last = pe.matmul(bank[32 * j:32 * j + 32, S * q:S * (q + 1)],
                                             qx[0:KA, buf, h0 + 4 * q + j, :], stk[0:KA, buf, h0 + 4 * q + j, 1, :],
                                             start=True, stop=True, skip_group_check=True)
                last.then_inc(max_scores, 1)

            def values_pass(g, quad):
                u, buf = g // 2, (g // 2) % 2
                i = HH * half_no[g] + 4 * quad
                if kind(u) == CLASS:
                    pe.wait_ge(exp_done, i + 4)
                else:
                    pe.wait_ge(masked, i // 4 + 1)
                if quad == 0:
                    wait_cleared(pe, "values", u)
                    if half_no[g] > 0:
                        pe.wait_ge(ot_ready, half_no[g])
                at = 0
                for t, a, b in SPANS[kind(u)]:
                    for j in range(4):
                        h = HH * (g % 2) + 4 * quad + j
                        last = pe.matmul(ps_v[32 * j:32 * j + 32, quad, a:b], vv[:, buf, t, h, :],
                                         pr[:, (i + j) % RING, at:at + b - a],
                                         start=(t == 0), stop=True, skip_group_check=True)
                    at += b - a
                last.then_inc(pv_done, 1)

            def run(task, u):
                bench = bank_of(task, u)
                bench16 = bench.bitcast(BF16)
                begin(task, u)
                if task == "lora_turn":
                    pe.wait_ge(w_lora, 16 * 12)
                    pe.wait_ge(ident_made, 2)
                    for i in range(4):
                        last = pe.transpose(bench[0:RANK, D * i:D * (i + 1)], lo_b[:, i, :], ident[:, :])
                elif task == "lora_merge":
                    wait_cleared(pe, "lora_turn", 0)
                    for i in range(4):
                        pe.matmul(bench[:, D * i:D * (i + 1)], wraw[:, i, :], ident[:, :],
                                  start=True, stop=False, skip_group_check=True)
                        last = pe.matmul(bench[:, D * i:D * (i + 1)], lo_a[:, i, :], lo_bt[:, i, :],
                                         start=False, stop=True, skip_group_check=True)
                elif task == "max_rows":
                    g = u
                    pe.wait_ge(max_parts, half_no[g] + 1)
                    for t in range(NT):
                        last = pe.transpose(bench16[0:3 * HH, P * t:P * (t + 1)],
                                            mp[:, g % 2, t].rearrange("p k h -> p (k h)"), identb[:, :])
                    if kind(g // 2) == CLASS:
                        last = pe.transpose(bench16[0:6, S:S + P], mpx[:, g % 2].rearrange("p k q -> p (k q)"),
                                            identb[:, :])
                elif task in ("turn_x", "turn_x3"):
                    v = u if task == "turn_x" else u + B + 2 + NU
                    pe.wait_ge(xn_ready, norm_order[v] + 1)
                    for t in range(NT):
                        last = pe.transpose(bench[:, P * t:P * (t + 1)], xn[:, t, :], ident[:, :])
                elif task == "turn_bias":
                    pe.wait_ge(dh_ready, 3)
                    for i in range(2):
                        last = pe.matmul(bench[:, i:i + 1], row_dh[0:1, i, :], ident[0:1, 0:1], start=True, stop=True)
                elif task == "turn_ctx":
                    pe.wait_ge(ctx_in, 16)
                    for t in range(NT):
                        last = pe.transpose(bench[:, P * t:P * (t + 1)], ct[:, UNITS[u][1], t, :], ident[:, :])
                elif task in ("qk", "qk3"):
                    if task == "qk":
                        st, xq = STG[kind(u)], xt[:, u % 2, :]
                        xk = cx[:, u % 2, :] if kind(u) == CROSS else xq
                        wait_cleared(pe, "turn_x", u)
                        if kind(u) == CROSS:
                            wait_cleared(pe, "turn_ctx", u)
                    else:
                        st, xq = 2, xt3[:, UNITS[u][1], :]
                        xk = xq
                        wait_cleared(pe, "turn_x3", u)
                    if st:
                        pe.wait_ge(w_in, 16 * 6)
                        pe.wait_ge(dh_ready, 3)
                    pe.matmul(bench[:, 0:S], w_dh[:, st, Q, :], xq, start=True, stop=True)
                    last = pe.matmul(bench[:, S:2 * S], w_dh[:, st, K, :], xk, start=True, stop=True)
                elif task == "q_tokens":
                    wait_cleared(pe, "turn_x3", u)
                    for t in range(NT):
                        last = pe.matmul(bench[:, P * t:P * (t + 1)], xt3[:, UNITS[u][1], P * t:P * (t + 1)],
                                         w[:, 2, Q, :], start=True, stop=True)
                elif task == "values":
                    k, b = UNITS[u]
                    src = {SELF: xt[:, u % 2, :], CROSS: cx[:, u % 2, :], CLASS: xt3[:, b, :]}[k]
                    if k == CLASS:
                        wait_cleared(pe, "turn_x3", u - B - 2)
                    else:
                        wait_cleared(pe, "turn_x" if k == SELF else "turn_ctx", u)
                    for t in range(NT):
                        last = pe.matmul(bench[:, P * t:P * (t + 1)], src[:, P * t:P * (t + 1)],
                                         w[:, STG[k], V_, :], start=True, stop=True)
                elif task == "turn_out":
                    g = u
                    pe.wait_ge(ot_ready, half_no[g] + 1)
                    for t in range(NT):
                        for q in range(2):
                            i = 2 * t + q
                            last = pe.transpose(bench[:, GV * i:GV * (i + 1)], ot[:, g % 2, q, P * t:P * (t + 1)],
                                                ident[:, :])
                elif task == "turn_heads":
                    wait_cleared(pe, "turn_out", 2 * u)
                    wait_cleared(pe, "turn_out", 2 * u + 1)
                    for t in range(NT):
                        last = pe.transpose(bench[:, P * t:P * (t + 1)], heads[:, t, :], ident[:, :])
                elif task == "project":
                    wait_cleared(pe, "turn_heads", u)
                    for t in range(NT):
                        last = pe.matmul(bench[:, P * t:P * (t + 1)], heads_t[:, P * t:P * (t + 1)],
                                         w[:, STG[kind(u)], O, :], start=True, stop=True)
                elif task == "reg_scores":
                    g = u
                    buf, h0 = (g // 2) % 2, HH * (g % 2)
                    for h in range(HH):
                        for t in range(NT):
                            i = NT * h + t
                            last = pe.matmul(bench[:, XC * i:XC * (i + 1)], stk[0:KB, buf, h0 + h, 1, P * t:P * (t + 1)],
                                             qx[0:KB, buf, h0 + h, 0:XC], start=True, stop=True)
                elif task == "reg_values":
                    g = u
                    buf, h0 = (g // 2) % 2, HH * (g % 2)
                    wait_cleared(pe, "reg_scores", g)
                    for q in range(2):
                        for t in range(NT):
                            for j in range(4):
                                last = pe.matmul(bench[32 * j:32 * j + 32, XC * q:XC * (q + 1)],
                                                 vv[:, buf, t, h0 + 4 * q + j, :], px[:, 4 * q + j, t, :],
                                                 start=(t == 0), stop=True, skip_group_check=True)
                elif task == "reg_turn":
                    wait_cleared(pe, "reg_values", u)
                    for q in range(2):
                        last = pe.transpose(bench[0:XC, GV * q:GV * (q + 1)], otx[:, q, :], ident[:, :])
                elif task == "turn_class":
                    pe.wait_ge(cls_ready, 1)
                    last = pe.transpose(bench16[0:4 * B * NT, 0:P], cls[:, :, :, :].rearrange("p k b t -> p (k b t)"),
                                        identb[:, :])
                last.then_inc(filled, 1)

            for task, u in SETUP_TASKS:
                run(task, u)
            pe.wait_ge(consts_made, 2)
            for g in SLOTS:
                for p in range(8):
                    if g in half_no:
                        second_pass(g, p)
                    if g + 2 in chunk_base:
                        for i, chunk in max_part(g + 2, p):
                            first_pass(g + 2, i, chunk)
                    if p == (AT0, AT1)[g % 2]["values_b"] and g - 1 in half_no:
                        values_pass(g - 1, 1)
                    if p == (AT0, AT1)[g % 2]["values_a"] and g in half_no:
                        values_pass(g, 0)
                    for task, u in bench_tasks(g, p):
                        run(task, u)

        @block.scalar
        def _(act):
            def ready(task, u):
                act.wait_ge(filled, turn(task, u) + 1)

            def run(task, u):
                bench = bank_of(task, u)
                bench16 = bench.bitcast(BF16)
                free = cleared[turn(task, u) % 2]
                if task == "lora_turn":
                    ready(task, u)
                    act.activation(lo_bt[:, :, :].rearrange("r a d -> r (a d)"), bench[0:RANK, :], ACT.Copy,
                                   scale=1.0 / RANK).then_inc(free, 1)
                elif task == "lora_merge":
                    ready(task, u)
                    act.activation(w_dh[:, 0].rearrange("p a (d h) -> p a h d", d=HD),
                                   bench[:, 0:2 * D].rearrange("p (a h d) -> p a h d", a=2, d=HD), ACT.Copy)
                    act.activation(w[:, 0, V_:, :].rearrange("p a d -> p (a d)"), bench[:, 2 * D:],
                                   ACT.Copy).then_inc(free, 1)
                elif task == "max_rows":
                    g = u
                    ready(task, g)
                    if g >= 2 and g - 2 in half_no:
                        act.wait_ge(max_stored, max_store_count(g - 2))
                    if kind(g // 2) == CLASS:
                        act.activation(mtx[:, g % 2, :], bench16[0:6, S:S + P], ACT.Copy)
                    act.activation(mt[:, g % 2, :], bench16[0:3 * HH, 0:S], ACT.Copy).then_inc(free, 1)
                elif task == "turn_x":
                    ready(task, u)
                    act.activation(xt[:, u % 2, :], bench[:, 0:S], ACT.Copy).then_inc(free, 1)
                elif task == "turn_x3":
                    ready(task, u)
                    act.activation(xt3[:, UNITS[u][1], :], bench[:, 0:S], ACT.Copy).then_inc(free, 1)
                elif task == "turn_bias":
                    ready(task, u)
                    act.activation(qk_bias[:, :], bench[:, 0:2], ACT.Copy).then_inc(free, 1)
                elif task == "turn_ctx":
                    ready(task, u)
                    act.activation(cx[:, u % 2, :], bench[:, 0:S], ACT.Copy).then_inc(free, 1)
                elif task in ("qk", "qk3"):
                    ready(task, u)
                    i = part_order[u + (B + 2 if task == "qk3" else 0)]
                    act.wait_ge(parts_stored, NSTORE * i)
                    first = parts[:, 0, :, :].rearrange("p a q -> p (a q)")
                    if task == "qk" and kind(u) == CROSS:
                        act.wait_ge(small_in, 16 * 8)
                        for a in range(2):
                            last = act.activation(parts[:, 0, a, :], bench[:, S * a:S * (a + 1)], ACT.Identity,
                                                  bias=qk_bias[:, a:a + 1])
                    else:
                        last = act.activation(first, bench[:, :], ACT.Copy)
                    last.then_inc(part1_ready, 1)
                elif task == "q_tokens":
                    ready(task, u)
                    act.wait_ge(stats3_ready, UNITS[u][1])
                    act.activation(sq[:, :], bench[:, 0:S], ACT.Square).then_inc(sq_ready, 1)
                elif task == "turn_heads":
                    ready(task, u)
                    act.activation(heads_t[:, :], bench[:, 0:S], ACT.Copy).then_inc(free, 1)
                elif task == "reg_scores":
                    ready(task, u)
                    act.activation(px[:, :, :, :].rearrange("p h t c -> p (h t c)"), bench[:, 0:HH * NT * XC],
                                   ACT.Exp, scale=SCALE).then_inc(free, 1)
                elif task == "reg_values":
                    ready(task, u)
                    act.activation(otx[:, :, :].rearrange("p q c -> p (q c)"), bench[:, 0:2 * XC],
                                   ACT.Copy).then_inc(free, 1)
                elif task == "turn_class":
                    ready(task, u)
                    act.activation(cls_t[:, :], bench16[0:4 * B * NT, 0:P], ACT.Copy).then_inc(free, 1)

            def second_part(u):
                wait_cleared(act, *part_task(u))
                act.activation(parts[:, 1, :, :], rest[:, :, :], ACT.Copy).then_inc(part2_ready, 1)

            def exponentials(g, c):
                i = HH * half_no[g] + c
                wd = WIDTH[kind(g // 2)]
                act.wait_ge(scores, i + 1)
                if i >= RING:
                    act.wait_ge(pv_done, (i - RING) // 4 + 1)
                act.activation(pr[:, i % RING, 0:wd], ps_b[:, i % 3, 0:wd], ACT.Exp, scale=SCALE).then_inc(exp_done, 1)

            def copy_out(g):
                act.wait_ge(pv_done, 2 * half_no[g] + 2)
                if half_no[g] >= 2:
                    act.wait_ge(filled, turn("turn_out", live_halves[half_no[g] - 2]) + 1)
                act.activation(ot[:, g % 2, :, :], ps_v[:, :, :], ACT.Copy).then_inc(ot_ready, 1)

            for task, u in SETUP_TASKS:
                run(task, u)
            for g in SLOTS:
                for p in range(8):
                    if g in half_no:
                        exponentials(g, p)
                    if p == (AT0, AT1)[g % 2]["copy_out"] and g - 1 in half_no:
                        copy_out(g - 1)
                    for task, u in bench_tasks(g, p):
                        run(task, u)
                    for what, u in part_tasks(g, p):
                        if what == "part2":
                            second_part(u)
                    if g == 2 * (CLASS0 - 2) + 1 and p == 6:
                        act.wait_ge(stats3_ready, B)
                        act.activation(rt[:, :, :], n2[:, :, :], ACT.Sqrt).then_inc(rn_ready, 1)

        @block.vector
        def _(dve):
            steps = [0]

            def link(ins):
                steps[0] += 1
                ins.then_inc(dve_step, 1)
                dve.wait_ge(dve_step, steps[0])

            def take_max(g, i, chunk):
                what, h1 = chunk
                no = chunk_base[g] + i
                dve.wait_ge(max_scores, no + 1)
                bank = ps_a[:, no % 2, :]
                m = nm[:, g % 2]
                if what == "reg":
                    src, dst = bank.rearrange("p (a k) -> p a k", a=2), nx[:, g % 2, :]
                elif what == "tile0":
                    src, dst = bank.rearrange("p (a k) -> p a k", a=4), m[:, 0, h1:h1 + 4]
                elif what == "tile1":
                    src, dst = bank.rearrange("p (a k) -> p a k", a=2), m[:, 1, h1:h1 + 2]
                elif what == "window":
                    src, dst = bank[:, 0:2 * WW].rearrange("p (a k) -> p a k", a=2), m[:, :, h1]
                else:
                    src, dst = bank.rearrange("p (a k) -> p a k", a=2), m[:, :, h1]
                dve.tensor_reduce(dst, src, AX.X, ALU.max, negate=True).then_inc(max_taken, 1)

            def split_max(g):
                m, k = nm[:, g % 2], mp[:, g % 2]
                dve.wait_ge(max_taken, chunk_base[g] + len(max_chunks(g)))
                if half_no[g] >= 2:
                    dve.wait_ge(filled, turn("max_rows", live_halves[half_no[g] - 2]) + 1)
                link(dve.tensor_copy(k[:, :, 0, :], m))
                if half_no[g] > 0:
                    dve.wait_ge(max_parts, half_no[g])
                link(dve.tensor_tensor(nmr[:, :, :], m, k[:, :, 0, :], ALU.subtract))
                link(dve.tensor_copy(k[:, :, 1, :], nmr[:, :, :]))
                last = dve.tensor_tensor(k[:, :, 2, :], nmr[:, :, :], k[:, :, 1, :], ALU.subtract)
                if kind(g // 2) == CLASS:
                    m, k = nx[:, g % 2, :], mpx[:, g % 2]
                    link(last)
                    link(dve.tensor_copy(k[:, 0, :], m))
                    link(dve.tensor_tensor(nxr[:, :], m, k[:, 0, :], ALU.subtract))
                    link(dve.tensor_copy(k[:, 1, :], nxr[:, :]))
                    last = dve.tensor_tensor(k[:, 2, :], nxr[:, :], k[:, 1, :], ALU.subtract)
                last.then_inc(max_parts, 1)

            def norm(what, u):
                i = norm_order[u]
                three = u >= NU
                b = UNITS[u - NU][1] if three else UNITS[u][1]
                if what == "stats":
                    if three:
                        wait_cleared(dve, "project", CROSS0 + b)
                    elif kind(u) == CROSS:
                        wait_cleared(dve, "project", b)
                    elif b == 0:
                        dve.wait_ge(x_first, 16)
                    else:
                        dve.wait_ge(x_rest, 16)
                    for t in range(NT):
                        link(dve.bn_stats(st6[:, t, :], xr[:, b, t, :]))
                    for t in range(NT):
                        link(dve.bn_aggr(mv[:, t, :], st6[:, t, :]))
                    if i > 0:
                        dve.wait_ge(rstd_ready, i)
                    dve.tensor_scalar(ve[:, :], mv[:, :, 1], EPS, None, ALU.add).then_inc(stats_ready, 1)
                else:
                    dve.wait_ge(rstd_ready, i + 1)
                    if i > 0:
                        before = [k for k in norm_order if norm_order[k] == i - 1][0]
                        task = ("turn_x3", before - NU - B - 2) if before >= NU else ("turn_x", before)
                        dve.wait_ge(filled, turn(*task) + 1)
                    for t in range(NT):
                        last = dve.tensor_scalar(xn[:, t, :], xr[:, b, t, :], mv[:, t, 0:1], rs[:, t:t + 1],
                                                 ALU.subtract, ALU.mult)
                    last.then_inc(xn_ready, 1)

            def ready(task, u):
                dve.wait_ge(filled, turn(task, u) + 1)

            def run(task, u):
                bench = bank_of(task, u)
                free = cleared[turn(task, u) % 2]
                if task in ("qk", "qk3"):
                    i = part_order[u + (B + 2 if task == "qk3" else 0)]
                    dve.wait_ge(part1_ready, i + 1)
                    if task == "qk" and kind(u) == CROSS:
                        for a in range(2):
                            last = dve.scalar_tensor_tensor(rest[:, a, :], bench[:, S * a:S * (a + 1)],
                                                            qk_bias[:, a:a + 1], parts[:, 0, a, :],
                                                            ALU.add, ALU.subtract)
                    else:
                        last = dve.tensor_tensor(rest[:, :, :].rearrange("p a q -> p (a q)"), bench[:, :],
                                                 parts[:, 0, :, :].rearrange("p a q -> p (a q)"), ALU.subtract)
                    last.then_inc(free, 1)
                elif task == "q_tokens":
                    b = UNITS[u][1]
                    dve.wait_ge(sq_ready, b + 1)
                    if b == 0:
                        dve.wait_ge(g_pow, 2)
                    for t in range(NT):
                        last = dve.tensor_tensor(dg[:, D * t:D * (t + 1)], bench[:, P * t:P * (t + 1)], g_hat[:, :], ALU.mult)
                    last.then_inc(free, 1)
                    wait_cleared(dve, task, u)
                    link(dve.tensor_reduce(dq[:, b, :], dg[:, :].rearrange("p (h d) -> p h d", d=HD), AX.X, ALU.add))
                    dve.tensor_reduce(n2[:, b, :], sq[:, :].rearrange("p (h d) -> p h d", d=HD), AX.X,
                                      ALU.add).then_inc(stats3_ready, 1)
                elif task == "values":
                    ready(task, u)
                    buf = u % 2
                    prev = unit_no[u] - 2
                    if prev >= 0:
                        dve.wait_ge(pv_done, 4 * (prev + 1))
                    else:
                        dve.wait_ge(vv_zero, 1)
                    if kind(u - 2) == CLASS:
                        dve.wait_ge(filled, turn("reg_values", 2 * (u - 2) + 1) + 1)
                    dst = vv[:, buf, :, :, 0:HD]
                    src = bench[:, 0:S].rearrange("p (t h d) -> p t h d", t=NT, d=HD)
                    if kind(u) == CROSS:
                        dve.wait_ge(small_in, 16 * 8)
                        for t in range(NT):
                            last = dve.tensor_tensor(dst[:, t], src[:, t],
                                                     v_bias[:, :].rearrange("p (h d) -> p h d", d=HD), ALU.add)
                    else:
                        last = dve.tensor_copy(dst, src)
                    last.then_inc(free, 1)
                elif task == "turn_out":
                    g = u
                    ready(task, g)
                    if g % 2 == 0 and live_halves.index(g) >= 2:
                        before = live_halves[half_no[g] - 2] // 2
                        dve.wait_ge(filled, turn("turn_heads", before) + 1)
                    v = bench[:, :].rearrange("p (x c) -> p x c", c=32)
                    h1 = HH * HD * (g % 2)
                    if half_no[g] > 0:
                        wait_cleared(dve, task, live_halves[half_no[g] - 1])
                    link(dve.reciprocal(rec[:, :], v[:, :, HD]))
                    dst = heads[:, :, h1:h1 + HH * HD].rearrange("p t (x d) -> p t x d", d=HD)
                    src = bench[:, :].rearrange("p (t x c) -> p t x c", t=NT, c=32)[:, :, :, 0:HD]
                    r = rec[:, :].rearrange("p (t x) -> p t x", t=NT).unsqueeze(3).broadcast_to([P, NT, HH, HD])
                    last = dve.tensor_tensor(dst, src, r, ALU.mult)
                    if kind(g // 2) == CLASS:
                        link(last)
                        wait_cleared(dve, "reg_turn", g)
                        a = heads[0:REG, 0, h1:h1 + HH * HD]
                        link(dve.tensor_tensor(a, a, hx[0:REG, g % 2, :], ALU.add))
                        last = dve.tensor_scalar(a, a, 0.5, None, ALU.mult)
                    last.then_inc(free, 1)
                elif task == "project":
                    ready(task, u)
                    b = UNITS[u][1]
                    if kind(u) != SELF:
                        dve.wait_ge(bias_added, bias_count(u + NU if kind(u) == CLASS else u))
                    dst = xr[:, b].rearrange("p t d -> p (t d)")
                    dve.tensor_tensor(dst, bench[:, 0:S], dst, ALU.add).then_inc(free, 1)
                elif task == "reg_turn":
                    g = u
                    ready(task, g)
                    v = bench[0:XC, 0:2 * GV].rearrange("p (x c) -> p x c", c=32)
                    if class_no(g) > 0:
                        wait_cleared(dve, task, g - 1)
                    link(dve.reciprocal(recx[:, :], v[:, :, HD]))
                    dve.tensor_tensor(hx[:, g % 2, :].rearrange("p (x d) -> p x d", d=HD), v[:, :, 0:HD],
                                      recx[:, :].unsqueeze(2).broadcast_to([XC, HH, HD]), ALU.mult).then_inc(free, 1)

            def third_part(u):
                dve.wait_ge(part2_ready, part_order[u] + 1)
                dve.tensor_tensor(parts[:, 2, :, :], rest[:, :, :], parts[:, 1, :, :],
                                  ALU.subtract).then_inc(parts_ready, 1)

            def classes():
                dve.wait_ge(rn_ready, 1)
                link(dve.reciprocal(rn[:, :, :], rt[:, :, :]))
                link(dve.tensor_tensor(sh[:, :, :], rn[:, :, :], rn[:, :, :], ALU.mult))
                link(dve.tensor_tensor(sh[:, :, :], sh[:, :, :], n2[:, :, :], ALU.mult))
                link(dve.tensor_scalar(sh[:, :, :], sh[:, :, :], -0.5, 1.5, ALU.mult, ALU.add))
                link(dve.tensor_tensor(rn[:, :, :], rn[:, :, :], sh[:, :, :], ALU.mult))
                link(dve.tensor_tensor(sh[:, :, :], dq[:, :, :], rn[:, :, :], ALU.mult))
                link(dve.tensor_reduce(sim[:, 2], sh[:, :, :].rearrange("p b (t h) -> p b t h", h=NH), AX.X, ALU.add))
                link(dve.tensor_scalar(sim[:, 0], sim[:, 2], 1.0 / NH, None, ALU.mult))
                link(dve.tensor_copy(sim[:, 1], sim[:, 0]))
                link(dve.tensor_scalar(sim[:, 2], sim[:, 0], -1.0, None, ALU.mult))
                link(dve.memset(sim[0:REG, 1:3, :, 0], -3.0e38))
                link(dve.tensor_reduce(ends[:, 0:1], sim[:, 1], AX.XY, ALU.max))
                dve.tensor_reduce(ends[:, 1:2], sim[:, 2], AX.XY, ALU.max).then_inc(ends_ready, 1)
                dve.wait_ge(ends_done, 1)
                link(dve.tensor_tensor(span[:, 0:1], ends_all[:, 0:1], ends_all[:, 1:2], ALU.add))
                link(dve.reciprocal(span[:, 1:2], span[:, 0:1]))
                link(dve.tensor_scalar(sim[:, 1], sim[:, 0], ends_all[:, 1:2], span[:, 1:2], ALU.add, ALU.mult))
                link(dve.tensor_scalar(pos[:, :, :], sim[:, 1], SIM_CUT, None, ALU.is_gt))
                link(dve.tensor_copy(cls[:, 0], pos[:, :, :]))
                link(dve.tensor_scalar(cls[:, 1], pos[:, :, :], -1.0, 1.0, ALU.mult, ALU.add))
                link(dve.tensor_scalar(cls[:, 2], pos[:, :, :], -MASKED, MASKED, ALU.mult, ALU.add))
                link(dve.tensor_scalar(cls[:, 3], pos[:, :, :], MASKED, None, ALU.mult))
                link(dve.memset(cls[0:REG, 0, :, 0], 0.0))
                link(dve.memset(cls[0:REG, 1, :, 0], 1.0))
                dve.memset(cls[0:REG, 2:4, :, 0], 0.0).then_inc(cls_ready, 1)

            for g in SLOTS:
                for p in range(8):
                    if g + 2 in chunk_base:
                        for i, chunk in max_part(g + 2, p):
                            take_max(g + 2, i, chunk)
                        if p == 7 and g + 2 in half_no:
                            split_max(g + 2)
                    for task, u in bench_tasks(g, p):
                        if task == "turn_class":
                            classes()
                        else:
                            run(task, u)
                    for what, u in part_tasks(g, p):
                        if what == "part3":
                            third_part(u)
                    for what, u in norm_tasks(g, p):
                        norm(what, u)

        @block.gpsimd
        def _(pool):
            steps = [0]

            def link(ins):
                steps[0] += 1
                ins.then_inc(pool_step, 1)
                pool.wait_ge(pool_step, steps[0])

            def mask(g, c):
                i = HH * half_no[g] + 4 * c
                k = kind(g // 2)
                pool.wait_ge(exp_done, i + 4)
                p = pr[:, i % RING:i % RING + 4]
                if k == SELF:
                    both = p.rearrange("p h (a q) -> p h a q", q=S)[:, :, :, 0:P]
                    pool.affine_select(out=both, in_=both, compare_op=ALU.is_ge, fill=0.0, base=0,
                                       pattern=[[0, 4], [0, 2], [1, P]], channel_multiplier=-1).then_inc(masked, 1)
                else:
                    for at, m, base, s in ((0, WIN, WIN, 1), (WIN, P, 0, -1), (WW, P, 0, 1), (WW + P, WIN, 0, -1)):
                        v = p[:, :, at:at + m]
                        last = pool.affine_select(out=v, in_=v, compare_op=ALU.is_ge, fill=0.0, base=base,
                                                  pattern=[[0, 4], [s, m]], channel_multiplier=-s)
                    last.then_inc(masked, 1)

            link(pool.memset(ident[:, :], 0.0))
            pool.affine_select(out=ident[:, :], in_=ident[:, :], compare_op=ALU.not_equal, fill=1.0, base=0,
                               pattern=[[-1, P]], channel_multiplier=1).then_inc(ident_made, 1)
            link(pool.memset(identb[:, :], 0.0))
            pool.affine_select(out=identb[:, :], in_=identb[:, :], compare_op=ALU.not_equal, fill=1.0, base=0,
                               pattern=[[-1, P]], channel_multiplier=1).then_inc(ident_made, 1)
            link(pool.memset(neg_half[:, :], -0.5))

            def reciprocal_deviation(i):
                pool.wait_ge(stats_ready, i + 1)
                if i > 0:
                    pool.wait_ge(xn_ready, i)
                pool.tensor_tensor(rs[:, :], ve[:, :], neg_half[:, 0:NT], ALU.pow).then_inc(rstd_ready, 1)

            def clear_stack(buf):
                link(pool.memset(stk[:, buf].rearrange("p h s q -> p (h s q)").bitcast(F32), 0.0))
                pool.memset(stk[MROW:P, buf, :, 1, :], 1.0).then_inc(stacks_zero, 1)
                pool.wait_ge(stacks_zero, buf + 1)

            clear_stack(0)
            reciprocal_deviation(0)
            link(pool.memset(mask_c[:, :, :], 0.0))
            link(pool.memset(mask_w[:, :, :], 0.0))
            pool.affine_select(out=mask_c[:, :, :], in_=mask_c[:, :, :], compare_op=ALU.is_ge, fill=MASKED, base=0,
                               pattern=[[0, 4], [-1, P]], channel_multiplier=1).then_inc(consts_made, 1)
            for t, b1, b2 in ((0, WIN, WIN), (1, 2 * WIN, 0)):
                v = mask_w[:, t, :]
                link(pool.affine_select(out=v, in_=v, compare_op=ALU.is_ge, fill=MASKED, base=b1,
                                        pattern=[[-1, WW]], channel_multiplier=1))
                last = pool.affine_select(out=v, in_=v, compare_op=ALU.is_ge, fill=MASKED, base=b2,
                                          pattern=[[1, WW]], channel_multiplier=-1)
            last.then_inc(consts_made, 1)
            link(pool.memset(vv[:, :, :, :, :], 0.0))
            pool.memset(vv[:, :, :, :, HD:HD + 1], 1.0).then_inc(vv_zero, 1)
            pool.memset(qx[:, :, :, :], 0.0).then_inc(qx_made, 1)
            link(pool.memset(qx_cls[:, :, :, :, :], 0.0))
            pool.memset(qx_cls[:, 0, :, :, 0:REG], 1.0).then_inc(qx_made, 1)
            pool.wait_ge(qx_made, 2)

            clear_stack(1)

            for g in SLOTS:
                n, h = g // 2, g % 2
                for p in range(8):
                    if p in (3, 7) and g in half_no and kind(g // 2) != CLASS:
                        mask(g, p // 4)
                    for what, u in norm_tasks(g, p):
                        i = norm_order[u]
                        if what == "stats":
                            if i > 0:
                                reciprocal_deviation(i)
                        elif u >= NU or kind(u) == CROSS:
                            three = u >= NU
                            b = UNITS[u - NU][1] if three else UNITS[u][1]
                            pool.wait_ge(xn_ready, i + 1)
                            pool.wait_ge(small_in, 16 * 8)
                            for t in range(NT):
                                v = xr[:, b, t, :]
                                last = pool.tensor_tensor(v, v, o_bias[:, 1 if three else 0, :], ALU.add)
                            last.then_inc(bias_added, 1)
                    if p == 0 and g + 2 in half_no and kind((g + 2) // 2) == CLASS:
                        gg = g + 2
                        buf, h0 = (gg // 2) % 2, HH * (gg % 2)
                        pool.wait_ge(stack_sem(gg), stack_count(gg))
                        if gg - 4 in half_no and kind((gg - 4) // 2) == CLASS:
                            pool.wait_ge(filled, turn("reg_scores", gg - 4) + 1)
                        pool.tensor_copy(qx[0:CLS, buf, h0:h0 + HH, 0:REG],
                                         stk[0:CLS, buf, h0:h0 + HH, 0, 0:REG]).then_inc(qx_ready, 1)
                if g == 3:
                    pool.wait_ge(w_in, 16 * 6)
                    pool.wait_ge(small_in, 16 * 8)
                    for dst, src in ((w_dh[:, 1], w[:, 1, 0:2]), (w_dh[:, 2], w[:, 2, 0:2]), (row_dh, qk_row)):
                        pool.tensor_copy(dst[:].rearrange("p a (d h) -> p a h d", d=HD),
                                         src[:].rearrange("p a (h d) -> p a h d", d=HD)).then_inc(dh_ready, 1)
                if g == 3:
                    pool.wait_ge(small_in, 16 * 8)
                    link(pool.tensor_tensor(g_sq[:, :], g_row[:, :], g_row[:, :], ALU.mult))
                    v = g_sq[:, :].rearrange("p (h d) -> p h d", d=HD)
                    link(pool.tensor_tensor(v[:, :, 0:4], v[:, :, 0:4], v[:, :, 4:8], ALU.add))
                    link(pool.tensor_tensor(v[:, :, 0:2], v[:, :, 0:2], v[:, :, 2:4], ALU.add))
                    link(pool.tensor_tensor(g_n2[:, :], v[:, :, 0], v[:, :, 1], ALU.add))
                    pool.tensor_tensor(g_rn[:, :], g_n2[:, :], neg_half[:, 0:NH], ALU.pow).then_inc(g_pow, 1)
                    pool.wait_ge(g_pow, 1)
                    pool.tensor_tensor(g_hat[:, :].rearrange("p (h d) -> p h d", d=HD),
                                       g_row[:, :].rearrange("p (h d) -> p h d", d=HD),
                                       g_rn[:, :].unsqueeze(2).broadcast_to([P, NH, HD]), ALU.mult).then_inc(g_pow, 1)
                if g == 2 * (CLASS0 - 2) + 1:
                    pool.wait_ge(ends_ready, 1)
                    pool.partition_all_reduce(ends_all[:, :], ends[:, :], P, RMAX).then_inc(ends_done, 1)


_INS = ['x', 'ctx_1024', 'L0_attn_wq', 'L0_attn_aq', 'L0_attn_bq', 'L0_attn_wk', 'L0_attn_ak', 'L0_attn_bk',
        'L0_attn_wv', 'L0_attn_av', 'L0_attn_bv', 'L0_attn_wo', 'L0_attn_ao', 'L0_attn_bo', 'L0_xattn_Wq',
        'L0_xattn_bq', 'L0_xattn_Wk', 'L0_xattn_bk', 'L0_xattn_Wv', 'L0_xattn_bv', 'L0_xattn_Wo', 'L0_xattn_bo',
        'L0_ffn_g_info', 'L0_ffn_W_qkv', 'L0_ffn_W_proj', 'L0_ffn_b_proj']
_OUTS = [((8, 256, 128), 'float32')]


def kernel(**inputs):
    import numpy as _np
    import concourse.bacc as _bacc
    from concourse import mybir as _mybir
    from concourse.bass_utils import run_bass_kernel_spmd as _run

    nc = _bacc.Bacc("TRN2", target_bir_lowering=False, num_devices=1)
    arrays, args = {}, []
    for name in _INS:
        a = _np.ascontiguousarray(inputs[name])
        arrays[f"in_{name}_dram"] = a
        args.append(nc.dram_tensor(f"in_{name}_dram", a.shape, _mybir.dt.from_np(a.dtype), kind="ExternalInput").ap())
    for i, (shape, dtype) in enumerate(_OUTS):
        dt = _mybir.dt.from_np(_np.dtype(dtype))
        args.append(nc.dram_tensor(f"out_{i}_dram", shape, dt, kind="ExternalOutput").ap())
    layer_kernel(nc, *args)
    r = _run(nc, [arrays], core_ids=[0])
    got = tuple(r.results[0][f"out_{i}_dram"] for i in range(len(_OUTS)))
    return got[0]
```

```python
from contextlib import ExitStack

import concourse.bass as bass
from concourse import mybir

F32 = mybir.dt.float32
BF16 = mybir.dt.bfloat16
ALU = mybir.AluOpType
ACT = mybir.ActivationFunctionType
AX = mybir.AxisListType
RMAX = bass.bass_isa.ReduceOp.max

SELF, CROSS, CLASS, IDLE = "self", "cross", "class", "idle"
Q, K, V_, O = range(4)
MASKED = -1.0e30
EPS = 1e-5
SIM_CUT = 0.9
REG = 5

TERMS = [(0, 2), (0, 1), (0, 0), (1, 0), (2, 0), (1, 1)]


def layer_kernel(nc: bass.Bass, x, ctx_1024, L0_attn_wq, L0_attn_aq, L0_attn_bq, L0_attn_wk, L0_attn_ak,
                 L0_attn_bk, L0_attn_wv, L0_attn_av, L0_attn_bv, L0_attn_wo, L0_attn_ao, L0_attn_bo,
                 L0_xattn_Wq, L0_xattn_bq, L0_xattn_Wk, L0_xattn_bk, L0_xattn_Wv, L0_xattn_bv, L0_xattn_Wo,
                 L0_xattn_bo, L0_ffn_g_info, L0_ffn_W_qkv, L0_ffn_W_proj, L0_ffn_b_proj, out):
    B, S, D = x.shape
    RANK = L0_attn_aq.shape[0]
    NH = 16
    HD = D // NH
    P = 128
    NT = S // P
    HH = NH // 2
    WIN = 64
    WW = P + WIN
    NTERM = len(TERMS)
    CLS = HD * NTERM
    MROW = 96
    KA = MROW
    KB = MROW + 3
    NM = NT * HH + 2
    RING = 12
    NSTORE = 16 * 6
    SCALE = float(HD) ** -0.5
    GV = 4 * 32
    ONE_PAIR = 1.0 + 0x3F80 / 2 ** 23
    XC = 8
    assert D == P and S == 2 * P and HD == 8

    UNITS = ([(SELF, b) for b in range(B)] + [(CROSS, b) for b in range(B)] + [(IDLE, 0)] * 2
             + [(CLASS, b) for b in range(B)])
    SPLIT_ON_POOL = (CLASS,)
    CROSS0, CLASS0, NU = B, 2 * B + 2, len(UNITS)

    def kind(u):
        return UNITS[u][0] if 0 <= u < NU else IDLE

    def live(u):
        return kind(u) != IDLE

    COS_GROUPS = ((0, B - 1), (B - 1, B))
    COS_AT = ((2 * (CLASS0 - 2) + 1, 1), (2 * (CLASS0 - 2) + 1, 3))

    STG = {SELF: 0, CROSS: 1, CLASS: 2}

    PLACES = {
        SELF: (
            dict(max_rows=1, turn_x=2, turn_ctx=1, qk=3, part2=5, part3=5, turn_out=4, turn_heads=6, project=7,
                 reg_scores=2, reg_turn=0, reg_values=6, stats3=7, copy_out=3, values_b=0, values_a=7),
            dict(max_rows=0, turn_x3=3, qk3=5, part2=4, part3=4, q_tokens=5, turn_out=5, values=7, reg_scores=5,
                 reg_turn=4, reg_values=7, scale3=1, stats=3, scale=7, copy_out=2, values_b=0, values_a=7)),
        CROSS: (
            dict(max_rows=0, turn_x=1, turn_ctx=1, qk=3, part2=5, part3=5, turn_out=4, turn_heads=6, project=7,
                 reg_scores=2, reg_turn=0, reg_values=6, stats3=7, copy_out=2, values_b=0, values_a=7),
            dict(max_rows=1, turn_x3=3, qk3=5, part2=6, part3=5, q_tokens=5, turn_out=7, values=6, reg_scores=5,
                 reg_turn=4, reg_values=7, scale3=1, stats=3, scale=7, copy_out=3, values_b=1, values_a=7)),
        CLASS: (
            dict(max_rows=0, turn_x=1, turn_ctx=1, qk=3, part2=5, part3=5, turn_out=4, turn_heads=6, project=7,
                 reg_scores=3, reg_turn=2, reg_values=5, stats3=7, copy_out=1, values_b=0, values_a=7),
            dict(max_rows=1, turn_x3=3, qk3=5, part2=6, part3=5, q_tokens=5, turn_out=7, values=5, reg_scores=4,
                 reg_turn=3, reg_values=6, scale3=1, stats=4, scale=7, copy_out=2, values_b=2, values_a=7)),
    }

    def places(g):
        k = SELF if g < 0 else CROSS if g < 2 * (CLASS0 - 1) and kind(g // 2) == IDLE else kind(g // 2)
        return PLACES[k if k != IDLE else CLASS][g % 2]

    def bench_tasks(g, p):
        n, h = g // 2, g % 2
        at = places(g)
        t = []
        if p == at["max_rows"] and live((g + 1) // 2):
            t.append(("max_rows", g + 1))
        if p == at["reg_scores"] and kind(n) == CLASS:
            t.append(("reg_scores", g))
        if p == at["reg_values"] and kind(n) == CLASS:
            t.append(("reg_values", g))
        if p == at["reg_turn"] and kind((g - 1) // 2) == CLASS:
            t.append(("reg_turn", g - 1))
        if h == 0:
            u = n + 2
            if p == at["turn_x"] and kind(u) in (SELF, CROSS):
                t.append(("turn_x", u))
            if p == at["turn_ctx"] and u == CROSS0:
                t.append(("turn_bias", 0))
            if p == at["turn_ctx"] and kind(u) == CROSS:
                t.append(("turn_ctx", u))
            if p == at["qk"] and kind(u) in (SELF, CROSS):
                t.append(("qk", u))
            if p == at["turn_out"] and live(n - 1):
                t.append(("turn_out", g - 1))
            if p == at["turn_heads"] and live(n - 1):
                t.append(("turn_heads", n - 1))
            if p == at["project"] and live(n - 1):
                t.append(("project", n - 1))
        else:
            if p == at["turn_x3"] and kind(n - 1) == CROSS:
                t.append(("turn_x3", n - 1))
            if p == at["qk3"] and kind(n - 1) == CROSS:
                t.append(("qk3", n - 1))
            if p == at["turn_x3" if n == CLASS0 - 2 else "q_tokens"] and kind(n - 1) == CROSS:
                t.append(("q_tokens", n - 1))
            if p == at["turn_out"] and live(n):
                t.append(("turn_out", g - 1))
            if p == at["values"] and live(n + 1):
                t.append(("values", n + 1))
            if p == 4 and n == CLASS0 - 2:
                t.append(("turn_class", 0))
        return t

    def part_tasks(g, p):
        n, h = g // 2, g % 2
        at = places(g)
        u = n + 2 if h == 0 and kind(n + 2) in (SELF, CROSS) else n - 1 + B + 2 if h == 1 and kind(n - 1) == CROSS else None
        return [(what, u) for what in ("part2", "part3") if u is not None and p == at[what]]

    FIRST, LAST = -5, 2 * NU + 2
    SLOTS = range(FIRST, LAST)
    SETUP_TASKS = [("lora_turn", 0), ("lora_merge", 0), ("lora_merge", 1)]
    bench_order, norm_order, part_order = {}, {}, {}
    for task in SETUP_TASKS:
        bench_order[task] = len(bench_order)
    for g in SLOTS:
        for p in range(8):
            for task in bench_tasks(g, p):
                bench_order[task] = len(bench_order)

    def norm_tasks(g, p):
        n, h = g // 2, g % 2
        t = []
        if h == 1 and kind(n - 1) == CROSS and p == places(g)["scale3"]:
            t.append(("scale", n - 1 + B + 2 + NU))
        if h == 0 and kind(n - 1) == CROSS and p == places(g)["stats3"]:
            t.append(("stats", n - 1 + B + 2 + NU))
        if h == 1 and kind(n + 3) in (SELF, CROSS):
            if p == places(g)["stats"]:
                t.append(("stats", n + 3))
            if p == places(g)["scale"]:
                t.append(("scale", n + 3))
        return t

    for g in SLOTS:
        for p in range(8):
            for what, u in norm_tasks(g, p):
                if what == "stats":
                    norm_order[u] = len(norm_order)
            for what, u in bench_tasks(g, p):
                if what in ("qk", "qk3"):
                    part_order[u + (B + 2 if what == "qk3" else 0)] = len(part_order)

    def turn(task, u):
        return bench_order[(task, u)]

    def max_chunks(g):
        if g < 0:
            return []
        k = kind(g // 2)
        if k == SELF:
            return ([("tile0", 4 * i) for i in range(HH // 4)] + [("tile1", 2 * i) for i in range(HH // 2)])
        if k == CROSS:
            return [("window", i) for i in range(HH)]
        if k == CLASS:
            return [("full", i) for i in range(HH)] + [("reg", 0)]
        return []

    chunk_base = {}
    total = 0
    for g in range(0, 2 * NU):
        chunk_base[g] = total
        total += len(max_chunks(g))

    def max_part(g, p):
        c = max_chunks(g)
        if g == 0:
            return [(i, c[i]) for i in range(len(c))] if p == 7 else []
        lo, hi = len(c) * p // 8, len(c) * (p + 1) // 8
        return [(i, c[i]) for i in range(lo, hi)]

    live_halves = [g for g in range(2 * NU) if live(g // 2)]
    half_no = {g: i for i, g in enumerate(live_halves)}
    unit_no = {u: half_no[2 * u] // 2 for u in range(NU) if live(u)}
    SPANS = {SELF: ((0, 0, S), (1, P, S)), CROSS: ((0, 0, WW), (1, S - WW, S)), CLASS: ((0, 0, S), (1, 0, S))}
    WIDTH = {SELF: S + P, CROSS: 2 * WW, CLASS: 2 * S}

    with ExitStack() as ctx:
        def sb(name, shape, dt=F32):
            return ctx.enter_context(nc.sbuf_tensor(name, shape, dt))

        def sem(name):
            return ctx.enter_context(nc.semaphore(name))

        xr = sb("xr", [P, B, NT, D])
        ct = sb("ct", [P, B, NT, D])
        w = sb("w", [P, 3, 4, D])
        w_dh = sb("w_dh", [P, 3, 2, D])
        row_dh = sb("row_dh", [1, 2, D])
        wraw = sb("wraw", [P, 4, D])
        lo_a = sb("lo_a", [RANK, 4, D])
        lo_b = sb("lo_b", [P, 4, RANK])
        lo_bt = sb("lo_bt", [RANK, 4, D])
        qk_row = sb("qk_row", [1, 2, D])
        qk_bias = sb("qk_bias", [P, 2])
        v_bias = sb("v_bias", [P, D])
        o_bias = sb("o_bias", [P, 2, D])
        g_row = sb("g_row", [P, D])
        g_sq = sb("g_sq", [P, D])
        g_n2 = sb("g_n2", [P, NH])
        g_rn = sb("g_rn", [P, NH])
        g_hat = sb("g_hat", [P, D])
        ident = sb("ident", [P, P])
        identb = sb("identb", [P, P], BF16)
        mask_c = sb("mask_c", [P, 4, P], BF16)
        mask_w = sb("mask_w", [P, NT, WW], BF16)
        neg_half = sb("neg_half", [P, NT * NH])
        stk = sb("stk", [P, 2, NH, 2, S], BF16)
        qx = sb("qx", [P, 2, NH, 32], BF16)
        qx_cls = sb("qx_cls", [1, 2, 2, NH, 32], BF16)
        pr = sb("pr", [P, RING, 2 * S])
        vv = sb("vv", [P, 2, NT, NH, 32])
        ot = sb("ot", [P, 2, 2, S])
        heads = sb("heads", [P, NT, D])
        heads_t = sb("heads_t", [P, S])
        rec = sb("rec", [P, NT * HH])
        st6 = sb("st6", [P, NT, 6])
        mv = sb("mv", [P, NT, 2])
        ve = sb("ve", [P, NT])
        rs = sb("rs", [P, NT])
        xn = sb("xn", [P, NT, D])
        xt = sb("xt", [P, 2, S])
        cx = sb("cx", [P, 2, S])
        xt3 = sb("xt3", [P, B, S])
        rest = sb("rest", [P, 2, S])
        parts = sb("parts", [P, 3, 2, S], BF16)
        nm = sb("nm", [P, 2, NM])
        nmr = sb("nmr", [P, NM])
        mp = sb("mp", [P, 2, 3 * NM], BF16)
        mt = sb("mt", [3 * NM, 2, P], BF16)
        px = sb("px", [P, HH, NT, XC])
        otx = sb("otx", [P, 2, XC])
        recx = sb("recx", [XC, HH])
        hx = sb("hx", [XC, 2, HH * HD])
        sq = sb("sq", [P, NT * D])
        dg = sb("dg", [P, NT * D])
        n2 = sb("n2", [P, B, NT * NH])
        dq = sb("dq", [P, B, NT * NH])
        rt = sb("rt", [P, B, NT * NH])
        rn = sb("rn", [P, B, NT * NH])
        sh = sb("sh", [P, B, NT * NH])
        cos_sum = sb("cos_sum", [P, B, NT])
        sim = sb("sim", [P, 3, B, NT])
        warm = sb("warm", [1, 1])
        ends = sb("ends", [P, 2])
        ends_all = sb("ends_all", [P, 2])
        span = sb("span", [P, 2])
        pos = sb("pos", [P, B, NT])
        cls = sb("cls", [P, 4, B, NT], BF16)
        cls_t = sb("cls_t", [4 * B * NT, P], BF16)

        ps_a = ctx.enter_context(nc.psum_tensor("ps_a", [P, 3, 512], F32))
        ps_b = ctx.enter_context(nc.psum_tensor("ps_b", [P, 2, 512], F32))
        ps_v = ctx.enter_context(nc.psum_tensor("ps_v", [P, 2, S], F32))
        bench_ps = ctx.enter_context(nc.psum_tensor("bench", [P, 2, 512], F32))

        part_scr = nc.dram_tensor("part_scr", (NU, NTERM, P, 2, S), BF16).ap()
        max_scr = nc.dram_tensor("max_scr", (2 * NU, 3 * NM, P), BF16).ap()
        cls_scr = nc.dram_tensor("cls_scr", (4, B * NT, P), BF16).ap()

        x_first, x_rest, ctx_in, w_in, small_in = map(
            sem, ["x_first", "x_rest", "ctx_in", "w_in", "small_in"])
        ident_made, consts_made, stacks_zero, qx_made, g_pow = map(
            sem, ["ident_made", "consts_made", "stacks_zero", "qx_made", "g_pow"])
        w_lora = [sem("w_lora_qk"), sem("w_lora_vo")]
        lo_b_in = sem("lo_b_in")
        dh_ready = sem("dh_ready")
        vv_zero = sem("vv_zero")
        pool_step, dve_step = sem("pool_step"), sem("dve_step")
        filled = sem("filled")
        cleared = [sem("cleared0"), sem("cleared1")]
        stats_ready, rstd_ready, xn_ready = map(sem, ["stats_ready", "rstd_ready", "xn_ready"])
        bias_added = sem("bias_added")
        part1_ready, part2_ready, parts_ready = map(sem, ["part1_ready", "part2_ready", "parts_ready"])
        parts_stored = sem("parts_stored")
        stack_ready = [sem(f"stack_ready{i}") for i in range(4)]
        qx_ready = sem("qx_ready")
        max_scores, max_taken, max_parts = map(sem, ["max_scores", "max_taken", "max_parts"])
        max_stored = sem("max_stored")
        max_ready = [sem("max_ready0"), sem("max_ready1")]
        scores, exp_done, masked = map(sem, ["scores", "exp_done", "masked"])
        pv_done, ot_ready = sem("pv_done"), sem("ot_ready")
        sq_ready, stats3_ready, rn_ready = map(sem, ["sq_ready", "stats3_ready", "rn_ready"])
        ends_ready, ends_done, cls_ready, cls_stored = map(
            sem, ["ends_ready", "ends_done", "cls_ready", "cls_stored"])
        stored = sem("stored")

        def bank_of(task, u):
            return bench_ps[:, turn(task, u) % 2, :]

        def wait_cleared(eng, task, u):
            k = turn(task, u)
            eng.wait_ge(cleared[k % 2], k // 2 + 1)

        def values_free(eng, u):
            prev = unit_no[u] - 2
            if prev >= 0:
                eng.wait_ge(pv_done, 4 * (prev + 1))
            else:
                eng.wait_ge(vv_zero, 1)
            if kind(u - 2) == CLASS:
                eng.wait_ge(filled, turn("reg_values", 2 * (u - 2) + 1) + 1)

        def maxima(g):
            return NM if kind(g // 2) == CLASS else NT * HH

        def split_max(eng, link, g):
            n = maxima(g)
            m, rest_m = nm[:, g % 2, 0:n], nmr[:, 0:n]
            k = mp[:, g % 2, 0:3 * n].rearrange("p (k m) -> p k m", k=3)
            eng.wait_ge(max_taken, chunk_base[g] + len(max_chunks(g)))
            if half_no[g] >= 2:
                eng.wait_ge(filled, turn("max_rows", live_halves[half_no[g] - 2]) + 1)
            link(eng.tensor_copy(k[:, 0], m))
            if half_no[g] > 0:
                eng.wait_ge(max_parts, half_no[g])
            link(eng.tensor_tensor(rest_m, m, k[:, 0], ALU.subtract))
            link(eng.tensor_copy(k[:, 1], rest_m))
            eng.tensor_tensor(k[:, 2], rest_m, k[:, 1], ALU.subtract).then_inc(max_parts, 1)

        def part_task(u):
            return ("qk3", u - B - 2) if kind(u) == CLASS else ("qk", u)

        def stack_sem(g):
            return stack_ready[g % 4]

        def stack_count(g):
            total = 0
            for gg in range(g % 4, g + 1, 4):
                if live(gg // 2):
                    total += 16 * (1 + (2 if kind(gg // 2) == CLASS else 0))
            return total

        def max_count(g):
            total = 0
            for gg in range(g % 2, g + 1, 2):
                if live(gg // 2):
                    total += 16 * (NT + 1 if kind(gg // 2) == CLASS else NT)
            return total

        CLASS_HALVES = [g for g in live_halves if kind(g // 2) == CLASS]

        def class_no(g):
            return CLASS_HALVES.index(g)

        def max_store_count(g):
            return 16 * sum(1 for gg in live_halves if gg <= g)

        def bias_count(u):
            return sum(1 for v, i in norm_order.items() if i <= norm_order[u] and (v >= NU or kind(v) == CROSS))

        block = ctx.enter_context(nc.Block())

        @block.sync
        def _(sp):
            def rows(v):
                return v.rearrange("(a n) -> a n", a=1)

            sp.dma_start(xr[:, 0], x[0].rearrange("(t p) d -> p t d", p=P)).then_inc(x_first, 16)
            for i, a in enumerate((L0_attn_bq, L0_attn_bk, L0_attn_bv, L0_attn_bo)):
                sp.dma_start(lo_b[:, i, :], a).then_inc(lo_b_in, 16)
            pairs = (((L0_attn_aq, L0_attn_wq), (L0_attn_ak, L0_attn_wk)),
                     ((L0_attn_av, L0_attn_wv), (L0_attn_ao, L0_attn_wo)))
            for k, pair in enumerate(pairs):
                for i, (a, w_full) in enumerate(pair, start=2 * k):
                    sp.dma_start(lo_a[:, i, :], a).then_inc(w_lora[k], 16)
                    sp.dma_start(wraw[:, i, :], w_full).then_inc(w_lora[k], 16)
            sp.dma_start(xr[:, 1:B].rearrange("p b t d -> p (b t) d"),
                         x[1:B].rearrange("b (t p) d -> p (b t) d", p=P)).then_inc(x_rest, 16)

            def stacks(g):
                u, h0, buf = g // 2, HH * (g % 2), (g // 2) % 2
                sp.wait_ge(parts_stored, NSTORE * (part_order[u] + 1))
                if g - 4 >= 0 and live((g - 4) // 2):
                    sp.wait_ge(scores, HH * (half_no[g - 4] + 1))
                if g < 4:
                    sp.wait_ge(stacks_zero, g // 2 + 1)
                if g - 4 >= 0 and kind((g - 4) // 2) == CLASS:
                    sp.wait_ge(filled, turn("reg_scores", g - 4) + 1)
                sp.dma_start(stk[0:CLS, buf, h0:h0 + HH],
                             part_scr[u].rearrange("t (d h) s q -> (t d) h s q", d=HD)[:, h0:h0 + HH]
                             ).then_inc(stack_sem(g), 16)

            def class_rows(g):
                u, h0, buf = g // 2, HH * (g % 2), (g // 2) % 2
                sp.wait_ge(cls_stored, 16)
                bb = UNITS[u][1]
                for s in range(2):
                    c = cls_scr[2 * s:2 * s + 2, NT * bb:NT * bb + NT, :].rearrange("k t q -> k (t q)")
                    c = c.unsqueeze(1).broadcast_to([2, HH, S])
                    sp.dma_start(stk[CLS:CLS + 2, buf, h0:h0 + HH, s, :], c).then_inc(stack_sem(g), 16)

            def max_rows(g):
                u, h0, buf = g // 2, HH * (g % 2), (g // 2) % 2
                wait_cleared(sp, "max_rows", g)
                n = maxima(g)
                sp.dma_start(max_scr[g, 0:3 * n], mt[0:3 * n, g % 2, :]).then_inc(max_stored, 16)
                sp.wait_ge(max_stored, max_store_count(g))
                m = max_scr[g, 0:3 * n].rearrange("(k m) q -> k m q", k=3)
                for t in range(NT):
                    sp.dma_start(stk[MROW:MROW + 3, buf, h0:h0 + HH, 0, P * t:P * (t + 1)],
                                 m[:, HH * t:HH * (t + 1)]).then_inc(max_ready[g % 2], 16)
                if kind(u) == CLASS:
                    c = m[:, NT * HH:].rearrange("k a c -> k (a c)").rearrange("k (h r) -> k h r", h=HH)
                    sp.dma_start(qx[MROW:MROW + 3, buf, h0:h0 + HH, :], c).then_inc(max_ready[g % 2], 16)

            def store_parts(u):
                for a, ready in enumerate((part1_ready, part2_ready, parts_ready)):
                    sp.wait_ge(ready, part_order[u] + 1)
                    for s in range(2):
                        at = [t for t in range(NTERM) if TERMS[t][s] == a]
                        step = at[1] - at[0] if len(at) > 1 else 1
                        dst = part_scr[u, at[0]:at[-1] + 1:step, :, s, :].rearrange("t r q -> r t q")
                        src = parts[:, a, s, :].unsqueeze(1).broadcast_to([P, len(at), S])
                        sp.dma_start(dst, src).then_inc(parts_stored, 16)

            def finish(b):
                wait_cleared(sp, "project", CLASS0 + b)
                sp.dma_start(out[b].rearrange("(t p) d -> p t d", p=P), xr[:, b]).then_inc(stored, 16)

            for g in SLOTS:
                n, h = g // 2, g % 2
                if g == -3:
                    sp.dma_start(ct[:, :, :, :].rearrange("p b t d -> p (b t) d"),
                                 ctx_1024.rearrange("b (t p) d -> p (b t) d", p=P)).then_inc(ctx_in, 16)
                if g == -2:
                    for i, a in enumerate((L0_xattn_Wq, L0_xattn_Wk, L0_xattn_Wv, L0_xattn_Wo)):
                        sp.dma_start(w[:, 1, i, :], a).then_inc(w_in, 16)
                    sp.dma_start(w[:, 2, 0:3, :], L0_ffn_W_qkv.rearrange("i (a o) -> i a o", a=3)).then_inc(w_in, 16)
                    sp.dma_start(w[:, 2, 3, :], L0_ffn_W_proj).then_inc(w_in, 16)
                if g == -1:
                    for i, a in enumerate((L0_xattn_bq, L0_xattn_bk)):
                        sp.dma_start(qk_row[0:1, i, :], rows(a)).then_inc(small_in, 16)
                    for dst, a in ((v_bias[:, :], rows(L0_xattn_bv)), (o_bias[:, 0, :], rows(L0_xattn_bo)),
                                   (o_bias[:, 1, :], rows(L0_ffn_b_proj)),
                                   (g_row[:, :], L0_ffn_g_info[0, 0:1, :])):
                        sp.dma_start(dst, a.broadcast_to([P, D])).then_inc(small_in, 16)
                if g == 3:
                    sp.wait_ge(qx_made, 2)
                    for k in range(2):
                        sp.dma_start(qx[CLS + k:CLS + k + 1], qx_cls[0:1, k]).then_inc(small_in, 16)
                if live((g + 1) // 2):
                    max_rows(g + 1)
                if 0 <= g + 3 and live((g + 3) // 2) and kind((g + 3) // 2) != CLASS:
                    stacks(g + 3)
                if n == CLASS0 - 2 and h == 1:
                    stacks(2 * CLASS0)
                    stacks(2 * CLASS0 + 1)
                    wait_cleared(sp, "turn_class", 0)
                    sp.dma_start(cls_scr.rearrange("k t q -> (k t) q"), cls_t[:, :]).then_inc(cls_stored, 16)
                    class_rows(2 * CLASS0)
                    class_rows(2 * CLASS0 + 1)
                elif kind((g + 3) // 2) == CLASS and g + 3 > 2 * CLASS0 + 1:
                    stacks(g + 3)
                    class_rows(g + 3)
                if h == 0 and kind(n + 2) in (SELF, CROSS):
                    store_parts(n + 2)
                if h == 1 and kind(n - 1) == CROSS:
                    store_parts(n - 1 + B + 2)
                if h == 1 and kind(n - 1) == CLASS:
                    finish(UNITS[n - 1][1])
            sp.wait_ge(stored, 16 * B)
            sp.wait_ge(parts_stored, NSTORE * 3 * B)
            sp.wait_ge(max_stored, max_store_count(2 * NU))

        @block.tensor
        def _(pe):
            def begin(task, u):
                k = turn(task, u)
                if k >= 2:
                    pe.wait_ge(cleared[k % 2], k // 2)

            def second_pass(g, c):
                u, buf, h = g // 2, (g // 2) % 2, HH * (g % 2) + c
                i = HH * half_no[g] + c
                if c == 0:
                    pe.wait_ge(max_ready[g % 2], max_count(g))
                if i >= 2:
                    pe.wait_ge(exp_done, i - 1)
                at = 0
                for t, a, b in SPANS[kind(u)]:
                    last = pe.matmul(ps_b[:, i % 2, at:at + b - a], stk[0:KB, buf, h, 1, t * P:(t + 1) * P],
                                     stk[0:KB, buf, h, 0, a:b], start=True, stop=True)
                    at += b - a
                last.then_inc(scores, 1)

            def first_pass(g, i, chunk):
                what, h1 = chunk
                u, buf, h0 = g // 2, (g // 2) % 2, HH * (g % 2)
                no = chunk_base[g] + i
                if i == 0:
                    pe.wait_ge(stack_sem(g), stack_count(g))
                if what == "reg":
                    pe.wait_ge(qx_ready, class_no(g) + 1)
                if no >= 3:
                    pe.wait_ge(max_taken, no - 2)
                bank = ps_a[:, no % 3, :]

                def part(dst, h, t, a, b, start):
                    return pe.matmul(dst, stk[0:KA, buf, h, 0, t * P:(t + 1) * P], stk[0:KA, buf, h, 1, a:b],
                                     start=start, stop=True, skip_group_check=True)

                if what == "tile0":
                    pe.matmul(bank, identb[:, :], mask_c[:, :, :].rearrange("p a b -> p (a b)"),
                              start=True, stop=False, skip_group_check=True)
                    for j in range(4):
                        last = part(bank[:, P * j:P * (j + 1)], h0 + h1 + j, 0, 0, P, False)
                elif what == "tile1":
                    pe.matmul(bank.rearrange("p (a b) -> p a b", a=2)[:, :, P:S], identb[:, :], mask_c[:, 0:2, :],
                              start=True, stop=False, skip_group_check=True)
                    for j in range(2):
                        last = part(bank[:, S * j:S * (j + 1)], h0 + h1 + j, 1, 0, S, False)
                elif what == "window":
                    pe.matmul(bank[:, 0:2 * WW], identb[:, :], mask_w[:, :, :].rearrange("p a b -> p (a b)"),
                              start=True, stop=False, skip_group_check=True)
                    for t in range(NT):
                        a = t * (S - WW)
                        last = part(bank[:, WW * t:WW * (t + 1)], h0 + h1, t, a, a + WW, False)
                elif what == "full":
                    for t in range(NT):
                        last = part(bank[:, S * t:S * (t + 1)], h0 + h1, t, 0, S, True)
                else:
                    for j in range(4):
                        for q in range(2):
                            last = pe.matmul(bank[32 * j:32 * j + 32, S * q:S * (q + 1)],
                                             qx[0:KA, buf, h0 + 4 * q + j, :], stk[0:KA, buf, h0 + 4 * q + j, 1, :],
                                             start=True, stop=True, skip_group_check=True)
                last.then_inc(max_scores, 1)

            def values_pass(g, quad):
                u, buf = g // 2, (g // 2) % 2
                i = HH * half_no[g] + 4 * quad
                if kind(u) == CLASS:
                    pe.wait_ge(exp_done, i + 4)
                else:
                    pe.wait_ge(masked, i // 4 + 1)
                if quad == 0:
                    wait_cleared(pe, "values", u)
                    if half_no[g] > 0:
                        pe.wait_ge(ot_ready, half_no[g])
                at = 0
                for t, a, b in SPANS[kind(u)]:
                    for j in range(4):
                        h = HH * (g % 2) + 4 * quad + j
                        last = pe.matmul(ps_v[32 * j:32 * j + 32, quad, a:b], vv[:, buf, t, h, :],
                                         pr[:, (i + j) % RING, at:at + b - a],
                                         start=(t == 0), stop=True, skip_group_check=True)
                    at += b - a
                last.then_inc(pv_done, 1)

            def run(task, u):
                bench = bank_of(task, u)
                bench16 = bench.bitcast(BF16)
                begin(task, u)
                if task == "lora_turn":
                    pe.wait_ge(lo_b_in, 16 * 4)
                    pe.wait_ge(ident_made, 2)
                    for i in range(4):
                        last = pe.transpose(bench[0:RANK, D * i:D * (i + 1)], lo_b[:, i, :], ident[:, :])
                elif task == "lora_merge":
                    pe.wait_ge(w_lora[u], 16 * 4)
                    wait_cleared(pe, "lora_turn", 0)
                    for i in (2 * u, 2 * u + 1):
                        pe.matmul(bench[:, D * i:D * (i + 1)], wraw[:, i, :], ident[:, :],
                                  start=True, stop=False, skip_group_check=True)
                        last = pe.matmul(bench[:, D * i:D * (i + 1)], lo_a[:, i, :], lo_bt[:, i, :],
                                         start=False, stop=True, skip_group_check=True)
                elif task == "max_rows":
                    g = u
                    pe.wait_ge(max_parts, half_no[g] + 1)
                    n = 3 * maxima(g)
                    last = pe.transpose(bench16[0:n, 0:P], mp[:, g % 2, 0:n], identb[:, :])
                elif task in ("turn_x", "turn_x3"):
                    v = u if task == "turn_x" else u + B + 2 + NU
                    pe.wait_ge(xn_ready, norm_order[v] + 1)
                    for t in range(NT):
                        last = pe.transpose(bench[:, P * t:P * (t + 1)], xn[:, t, :], ident[:, :])
                elif task == "turn_bias":
                    pe.wait_ge(dh_ready, 3)
                    for i in range(2):
                        last = pe.matmul(bench[:, i:i + 1], row_dh[0:1, i, :], ident[0:1, 0:1], start=True, stop=True)
                elif task == "turn_ctx":
                    pe.wait_ge(ctx_in, 16)
                    for t in range(NT):
                        last = pe.transpose(bench[:, P * t:P * (t + 1)], ct[:, UNITS[u][1], t, :], ident[:, :])
                elif task in ("qk", "qk3"):
                    if task == "qk":
                        st, xq = STG[kind(u)], xt[:, u % 2, :]
                        xk = cx[:, u % 2, :] if kind(u) == CROSS else xq
                        wait_cleared(pe, "turn_x", u)
                        if kind(u) == CROSS:
                            wait_cleared(pe, "turn_ctx", u)
                    else:
                        st, xq = 2, xt3[:, UNITS[u][1], :]
                        xk = xq
                        wait_cleared(pe, "turn_x3", u)
                    if st:
                        pe.wait_ge(w_in, 16 * 6)
                        pe.wait_ge(dh_ready, 3)
                    pe.matmul(bench[:, 0:S], w_dh[:, st, Q, :], xq, start=True, stop=True)
                    last = pe.matmul(bench[:, S:2 * S], w_dh[:, st, K, :], xk, start=True, stop=True)
                elif task == "q_tokens":
                    wait_cleared(pe, "turn_x3", u)
                    for t in range(NT):
                        last = pe.matmul(bench[:, P * t:P * (t + 1)], xt3[:, UNITS[u][1], P * t:P * (t + 1)],
                                         w[:, 2, Q, :], start=True, stop=True)
                elif task == "values":
                    k, b = UNITS[u]
                    src = {SELF: xt[:, u % 2, :], CROSS: cx[:, u % 2, :], CLASS: xt3[:, b, :]}[k]
                    if k == CLASS:
                        wait_cleared(pe, "turn_x3", u - B - 2)
                    else:
                        wait_cleared(pe, "turn_x" if k == SELF else "turn_ctx", u)
                    for t in range(NT):
                        last = pe.matmul(bench[:, P * t:P * (t + 1)], src[:, P * t:P * (t + 1)],
                                         w[:, STG[k], V_, :], start=True, stop=True)
                elif task == "turn_out":
                    g = u
                    pe.wait_ge(ot_ready, half_no[g] + 1)
                    for t in range(NT):
                        for q in range(2):
                            i = 2 * t + q
                            last = pe.transpose(bench[:, GV * i:GV * (i + 1)], ot[:, g % 2, q, P * t:P * (t + 1)],
                                                ident[:, :])
                elif task == "turn_heads":
                    wait_cleared(pe, "turn_out", 2 * u)
                    wait_cleared(pe, "turn_out", 2 * u + 1)
                    for t in range(NT):
                        last = pe.transpose(bench[:, P * t:P * (t + 1)], heads[:, t, :], ident[:, :])
                elif task == "project":
                    wait_cleared(pe, "turn_heads", u)
                    for t in range(NT):
                        last = pe.matmul(bench[:, P * t:P * (t + 1)], heads_t[:, P * t:P * (t + 1)],
                                         w[:, STG[kind(u)], O, :], start=True, stop=True)
                elif task == "reg_scores":
                    g = u
                    buf, h0 = (g // 2) % 2, HH * (g % 2)
                    for h in range(HH):
                        for t in range(NT):
                            i = NT * h + t
                            last = pe.matmul(bench[:, XC * i:XC * (i + 1)], stk[0:KB, buf, h0 + h, 1, P * t:P * (t + 1)],
                                             qx[0:KB, buf, h0 + h, 0:XC], start=True, stop=True)
                elif task == "reg_values":
                    g = u
                    buf, h0 = (g // 2) % 2, HH * (g % 2)
                    wait_cleared(pe, "reg_scores", g)
                    for q in range(2):
                        for t in range(NT):
                            for j in range(4):
                                last = pe.matmul(bench[32 * j:32 * j + 32, XC * q:XC * (q + 1)],
                                                 vv[:, buf, t, h0 + 4 * q + j, :], px[:, 4 * q + j, t, :],
                                                 start=(t == 0), stop=True, skip_group_check=True)
                elif task == "reg_turn":
                    wait_cleared(pe, "reg_values", u)
                    for q in range(2):
                        last = pe.transpose(bench[0:XC, GV * q:GV * (q + 1)], otx[:, q, :], ident[:, :])
                elif task == "turn_class":
                    pe.wait_ge(cls_ready, 1)
                    last = pe.transpose(bench16[0:4 * B * NT, 0:P], cls[:, :, :, :].rearrange("p k b t -> p (k b t)"),
                                        identb[:, :])
                last.then_inc(filled, 1)

            for task, u in SETUP_TASKS:
                run(task, u)
            pe.wait_ge(consts_made, 2)
            for g in SLOTS:
                for p in range(8):
                    if g in half_no:
                        second_pass(g, p)
                    if g + 2 in chunk_base:
                        for i, chunk in max_part(g + 2, p):
                            first_pass(g + 2, i, chunk)
                    if p == places(g)["values_b"] and g - 1 in half_no:
                        values_pass(g - 1, 1)
                    if p == places(g)["values_a"] and g in half_no:
                        values_pass(g, 0)
                    for task, u in bench_tasks(g, p):
                        run(task, u)

        @block.scalar
        def _(act):
            def ready(task, u):
                act.wait_ge(filled, turn(task, u) + 1)

            def run(task, u):
                bench = bank_of(task, u)
                bench16 = bench.bitcast(BF16)
                free = cleared[turn(task, u) % 2]
                if task == "lora_turn":
                    ready(task, u)
                    act.activation(lo_bt[:, :, :].rearrange("r a d -> r (a d)"), bench[0:RANK, :], ACT.Copy,
                                   scale=1.0 / RANK).then_inc(free, 1)
                elif task == "lora_merge":
                    ready(task, u)
                    if u == 0:
                        last = act.activation(w_dh[:, 0].rearrange("p a (d h) -> p a h d", d=HD),
                                              bench[:, 0:2 * D].rearrange("p (a h d) -> p a h d", a=2, d=HD),
                                              ACT.Copy)
                    else:
                        last = act.activation(w[:, 0, V_:, :].rearrange("p a d -> p (a d)"), bench[:, 2 * D:],
                                              ACT.Copy)
                    last.then_inc(free, 1)
                elif task == "max_rows":
                    g = u
                    ready(task, g)
                    if g >= 2 and g - 2 in half_no:
                        act.wait_ge(max_stored, max_store_count(g - 2))
                    n = 3 * maxima(g)
                    act.activation(mt[0:n, g % 2, :], bench16[0:n, 0:P], ACT.Copy).then_inc(free, 1)
                elif task == "turn_x":
                    ready(task, u)
                    act.activation(xt[:, u % 2, :], bench[:, 0:S], ACT.Copy).then_inc(free, 1)
                elif task == "turn_x3":
                    ready(task, u)
                    act.activation(xt3[:, UNITS[u][1], :], bench[:, 0:S], ACT.Copy).then_inc(free, 1)
                elif task == "turn_bias":
                    ready(task, u)
                    act.activation(qk_bias[:, :], bench[:, 0:2], ACT.Copy).then_inc(free, 1)
                elif task == "turn_ctx":
                    ready(task, u)
                    act.activation(cx[:, u % 2, :], bench[:, 0:S], ACT.Copy).then_inc(free, 1)
                elif task in ("qk", "qk3"):
                    ready(task, u)
                    i = part_order[u + (B + 2 if task == "qk3" else 0)]
                    act.wait_ge(parts_stored, NSTORE * i)
                    first = parts[:, 0, :, :].rearrange("p a q -> p (a q)")
                    if task == "qk" and kind(u) == CROSS:
                        act.wait_ge(small_in, 16 * 8)
                        for a in range(2):
                            last = act.activation(parts[:, 0, a, :], bench[:, S * a:S * (a + 1)], ACT.Identity,
                                                  bias=qk_bias[:, a:a + 1])
                    else:
                        last = act.activation(first, bench[:, :], ACT.Copy)
                    last.then_inc(part1_ready, 1)
                elif task == "q_tokens":
                    ready(task, u)
                    act.wait_ge(stats3_ready, UNITS[u][1])
                    act.activation(sq[:, :], bench[:, 0:S], ACT.Square).then_inc(sq_ready, 1)
                elif task == "values" and kind(u) != CROSS:
                    ready(task, u)
                    values_free(act, u)
                    act.activation(vv[:, u % 2, :, :, 0:HD],
                                   bench[:, 0:S].rearrange("p (t h d) -> p t h d", t=NT, d=HD),
                                   ACT.Copy).then_inc(free, 1)
                elif task == "turn_heads":
                    ready(task, u)
                    act.activation(heads_t[:, :], bench[:, 0:S], ACT.Copy).then_inc(free, 1)
                elif task == "reg_scores":
                    ready(task, u)
                    act.activation(px[:, :, :, :].rearrange("p h t c -> p (h t c)"), bench[:, 0:HH * NT * XC],
                                   ACT.Exp, scale=SCALE).then_inc(free, 1)
                elif task == "reg_values":
                    ready(task, u)
                    act.activation(otx[:, :, :].rearrange("p q c -> p (q c)"), bench[:, 0:2 * XC],
                                   ACT.Copy).then_inc(free, 1)
                elif task == "turn_class":
                    ready(task, u)
                    act.activation(cls_t[:, :], bench16[0:4 * B * NT, 0:P], ACT.Copy).then_inc(free, 1)

            def second_part(u):
                wait_cleared(act, *part_task(u))
                act.activation(parts[:, 1, :, :], rest[:, :, :], ACT.Copy).then_inc(part2_ready, 1)

            def exponentials(g, c):
                i = HH * half_no[g] + c
                wd = WIDTH[kind(g // 2)]
                act.wait_ge(scores, i + 1)
                if i >= RING:
                    act.wait_ge(pv_done, (i - RING) // 4 + 1)
                act.activation(pr[:, i % RING, 0:wd], ps_b[:, i % 2, 0:wd], ACT.Exp, scale=SCALE).then_inc(exp_done, 1)

            def copy_out(g):
                act.wait_ge(pv_done, 2 * half_no[g] + 2)
                if half_no[g] >= 2:
                    act.wait_ge(filled, turn("turn_out", live_halves[half_no[g] - 2]) + 1)
                act.activation(ot[:, g % 2, :, :], ps_v[:, :, :], ACT.Copy).then_inc(ot_ready, 1)

            for task, u in SETUP_TASKS:
                run(task, u)
            for g in SLOTS:
                for p in range(8):
                    if g in half_no:
                        exponentials(g, p)
                    if p == places(g)["copy_out"] and g - 1 in half_no:
                        copy_out(g - 1)
                    for task, u in bench_tasks(g, p):
                        run(task, u)
                    for what, u in part_tasks(g, p):
                        if what == "part2":
                            second_part(u)
                    if (g, p) in COS_AT:
                        g0, g1 = COS_GROUPS[COS_AT.index((g, p))]
                        act.wait_ge(stats3_ready, g1)
                        act.activation(rt[:, g0:g1], n2[:, g0:g1], ACT.Sqrt).then_inc(rn_ready, 1)
                        if g1 == B:
                            act.activation(warm[:, :], ident[0:1, 0:1], ACT.Exp)

        @block.vector
        def _(dve):
            steps = [0]

            def link(ins):
                steps[0] += 1
                ins.then_inc(dve_step, 1)
                dve.wait_ge(dve_step, steps[0])

            def take_max(g, i, chunk):
                what, h1 = chunk
                no = chunk_base[g] + i
                dve.wait_ge(max_scores, no + 1)
                bank = ps_a[:, no % 3, :]
                m = nm[:, g % 2, 0:NT * HH].rearrange("p (t h) -> p t h", h=HH)
                if i == 0 and half_no[g] >= 2:
                    dve.wait_ge(max_parts, half_no[g] - 1)
                if what == "reg":
                    src, dst = bank.rearrange("p (a k) -> p a k", a=2), nm[:, g % 2, NT * HH:]
                elif what == "tile0":
                    src, dst = bank.rearrange("p (a k) -> p a k", a=4), m[:, 0, h1:h1 + 4]
                elif what == "tile1":
                    src, dst = bank.rearrange("p (a k) -> p a k", a=2), m[:, 1, h1:h1 + 2]
                elif what == "window":
                    src, dst = bank[:, 0:2 * WW].rearrange("p (a k) -> p a k", a=2), m[:, :, h1]
                else:
                    src, dst = bank.rearrange("p (a k) -> p a k", a=2), m[:, :, h1]
                dve.tensor_reduce(dst, src, AX.X, ALU.max, negate=True).then_inc(max_taken, 1)

            def norm(what, u):
                i = norm_order[u]
                three = u >= NU
                b = UNITS[u - NU][1] if three else UNITS[u][1]
                if what == "stats":
                    if three:
                        wait_cleared(dve, "project", CROSS0 + b)
                    elif kind(u) == CROSS:
                        wait_cleared(dve, "project", b)
                    elif b == 0:
                        dve.wait_ge(x_first, 16)
                    else:
                        dve.wait_ge(x_rest, 16)
                    for t in range(NT):
                        last = dve.bn_stats(st6[:, t, :], xr[:, b, t, :])
                    link(last)
                    for t in range(NT):
                        last = dve.bn_aggr(mv[:, t, :], st6[:, t, :])
                    link(last)
                    if i > 0:
                        dve.wait_ge(rstd_ready, i)
                    dve.tensor_scalar(ve[:, :], mv[:, :, 1], EPS, None, ALU.add).then_inc(stats_ready, 1)
                else:
                    dve.wait_ge(rstd_ready, i + 1)
                    if i > 0:
                        before = [k for k in norm_order if norm_order[k] == i - 1][0]
                        task = ("turn_x3", before - NU - B - 2) if before >= NU else ("turn_x", before)
                        dve.wait_ge(filled, turn(*task) + 1)
                    for t in range(NT):
                        last = dve.tensor_scalar(xn[:, t, :], xr[:, b, t, :], mv[:, t, 0:1], rs[:, t:t + 1],
                                                 ALU.subtract, ALU.mult)
                    last.then_inc(xn_ready, 1)

            def ready(task, u):
                dve.wait_ge(filled, turn(task, u) + 1)

            def run(task, u):
                bench = bank_of(task, u)
                free = cleared[turn(task, u) % 2]
                if task in ("qk", "qk3"):
                    i = part_order[u + (B + 2 if task == "qk3" else 0)]
                    dve.wait_ge(part1_ready, i + 1)
                    if task == "qk" and kind(u) == CROSS:
                        for a in range(2):
                            last = dve.scalar_tensor_tensor(rest[:, a, :], bench[:, S * a:S * (a + 1)],
                                                            qk_bias[:, a:a + 1], parts[:, 0, a, :],
                                                            ALU.add, ALU.subtract)
                    else:
                        last = dve.tensor_tensor(rest[:, :, :].rearrange("p a q -> p (a q)"), bench[:, :],
                                                 parts[:, 0, :, :].rearrange("p a q -> p (a q)"), ALU.subtract)
                    last.then_inc(free, 1)
                elif task == "q_tokens":
                    b = UNITS[u][1]
                    dve.wait_ge(sq_ready, b + 1)
                    if b == 0:
                        dve.wait_ge(g_pow, 2)
                    for t in range(NT):
                        last = dve.tensor_tensor(dg[:, D * t:D * (t + 1)], bench[:, P * t:P * (t + 1)], g_hat[:, :], ALU.mult)
                    last.then_inc(free, 1)
                    wait_cleared(dve, task, u)
                    link(dve.tensor_reduce(dq[:, b, :], dg[:, :].rearrange("p (h d) -> p h d", d=HD), AX.X, ALU.add))
                    dve.tensor_reduce(n2[:, b, :], sq[:, :].rearrange("p (h d) -> p h d", d=HD), AX.X,
                                      ALU.add).then_inc(stats3_ready, 1)
                elif task == "values":
                    if kind(u) != CROSS:
                        return
                    ready(task, u)
                    values_free(dve, u)
                    dve.wait_ge(small_in, 16 * 8)
                    for t in range(NT):
                        last = dve.tensor_tensor(vv[:, u % 2, t, :, 0:HD],
                                                 bench[:, P * t:P * (t + 1)].rearrange("p (h d) -> p h d", d=HD),
                                                 v_bias[:, :].rearrange("p (h d) -> p h d", d=HD), ALU.add)
                    last.then_inc(free, 1)
                elif task == "turn_out":
                    g = u
                    ready(task, g)
                    if g % 2 == 0 and live_halves.index(g) >= 2:
                        before = live_halves[half_no[g] - 2] // 2
                        dve.wait_ge(filled, turn("turn_heads", before) + 1)
                    v = bench[:, :].rearrange("p (x c) -> p x c", c=32)
                    h1 = HH * HD * (g % 2)
                    if half_no[g] > 0:
                        wait_cleared(dve, task, live_halves[half_no[g] - 1])
                    link(dve.reciprocal(rec[:, :], v[:, :, HD]))
                    dst = heads[:, :, h1:h1 + HH * HD].rearrange("p t (x d) -> p t x d", d=HD)
                    src = bench[:, :].rearrange("p (t x c) -> p t x c", t=NT, c=32)[:, :, :, 0:HD]
                    r = rec[:, :].rearrange("p (t x) -> p t x", t=NT).unsqueeze(3).broadcast_to([P, NT, HH, HD])
                    last = dve.tensor_tensor(dst, src, r, ALU.mult)
                    if kind(g // 2) == CLASS:
                        link(last)
                        wait_cleared(dve, "reg_turn", g)
                        a = heads[0:REG, 0, h1:h1 + HH * HD]
                        last = dve.scalar_tensor_tensor(a, a, 0.5, hx[0:REG, g % 2, :], ALU.mult, ALU.add)
                    last.then_inc(free, 1)
                elif task == "project":
                    ready(task, u)
                    b = UNITS[u][1]
                    if kind(u) != SELF:
                        dve.wait_ge(bias_added, bias_count(u + NU if kind(u) == CLASS else u))
                    dst = xr[:, b].rearrange("p t d -> p (t d)")
                    dve.tensor_tensor(dst, bench[:, 0:S], dst, ALU.add).then_inc(free, 1)
                elif task == "reg_turn":
                    g = u
                    ready(task, g)
                    v = bench[0:XC, 0:2 * GV].rearrange("p (x c) -> p x c", c=32)
                    if class_no(g) > 0:
                        wait_cleared(dve, task, g - 1)
                    link(dve.reciprocal(recx[:, :], v[:, :, HD]))
                    dve.scalar_tensor_tensor(hx[:, g % 2, :].rearrange("p (x d) -> p x d", d=HD), v[:, :, 0:HD], 0.5,
                                             recx[:, :].unsqueeze(2).broadcast_to([XC, HH, HD]),
                                             ALU.mult, ALU.mult).then_inc(free, 1)

            def third_part(u):
                dve.wait_ge(part2_ready, part_order[u] + 1)
                dve.tensor_tensor(parts[:, 2, :, :], rest[:, :, :], parts[:, 1, :, :],
                                  ALU.subtract).then_inc(parts_ready, 1)

            def cosines(k):
                g0, g1 = COS_GROUPS[k]
                dve.wait_ge(rn_ready, k + 1)
                n2_, rn_, sh_ = n2[:, g0:g1], rn[:, g0:g1], sh[:, g0:g1]
                link(dve.reciprocal(rn_, rt[:, g0:g1]))
                link(dve.tensor_tensor(sh_, rn_, rn_, ALU.mult))
                link(dve.tensor_tensor(sh_, sh_, n2_, ALU.mult))
                link(dve.tensor_scalar(sh_, sh_, -0.5, 1.5, ALU.mult, ALU.add))
                link(dve.tensor_tensor(rn_, rn_, sh_, ALU.mult))
                link(dve.tensor_tensor(sh_, dq[:, g0:g1], rn_, ALU.mult))
                total_ = cos_sum[:, g0:g1]
                link(dve.tensor_reduce(total_, sh_.rearrange("p b (t h) -> p b t h", h=NH), AX.X, ALU.add))
                dve.tensor_scalar(sim[:, 0, g0:g1], total_, 1.0 / NH, None, ALU.mult)
                dve.tensor_scalar(sim[:, 1, g0:g1], total_, 1.0 / NH, None, ALU.mult)
                link(dve.tensor_scalar(sim[:, 2, g0:g1], total_, -1.0 / NH, None, ALU.mult))
                link(dve.memset(sim[0:REG, 1:3, g0:g1, 0], -3.0e38))

            def classes():
                dve.tensor_reduce(ends[:, 0:1], sim[:, 1], AX.XY, ALU.max)
                dve.tensor_reduce(ends[:, 1:2], sim[:, 2], AX.XY, ALU.max).then_inc(ends_ready, 1)
                dve.wait_ge(ends_done, 1)
                link(dve.tensor_tensor(span[:, 0:1], ends_all[:, 0:1], ends_all[:, 1:2], ALU.add))
                link(dve.reciprocal(span[:, 1:2], span[:, 0:1]))
                link(dve.tensor_scalar(sim[:, 1], sim[:, 0], ends_all[:, 1:2], span[:, 1:2], ALU.add, ALU.mult))
                link(dve.tensor_scalar(pos[:, :, :], sim[:, 1], SIM_CUT, None, ALU.is_gt))
                dve.tensor_copy(cls[:, 0], pos[:, :, :])
                dve.tensor_scalar(cls[:, 1], pos[:, :, :], -1.0, 1.0, ALU.mult, ALU.add)
                dve.tensor_scalar(cls[:, 2], pos[:, :, :], -MASKED, MASKED, ALU.mult, ALU.add)
                link(dve.tensor_scalar(cls[:, 3], pos[:, :, :], MASKED, None, ALU.mult))
                dve.memset(cls[0:REG, 0, :, 0], 0.0)
                dve.memset(cls[0:REG, 1, :, 0], 1.0)
                dve.memset(cls[0:REG, 2:4, :, 0], 0.0).then_inc(cls_ready, 1)

            for g in SLOTS:
                for p in range(8):
                    if g + 2 in chunk_base:
                        for i, chunk in max_part(g + 2, p):
                            take_max(g + 2, i, chunk)
                        if p == 7 and g + 2 in half_no and kind((g + 2) // 2) not in SPLIT_ON_POOL:
                            split_max(dve, link, g + 2)
                    for task, u in bench_tasks(g, p):
                        run(task, u)
                    for what, u in part_tasks(g, p):
                        if what == "part3":
                            third_part(u)
                    for what, u in norm_tasks(g, p):
                        norm(what, u)
                    if (g, p) in COS_AT:
                        cosines(COS_AT.index((g, p)))
                        if (g, p) == COS_AT[-1]:
                            classes()

        @block.gpsimd
        def _(pool):
            steps = [0]

            def link(ins):
                steps[0] += 1
                ins.then_inc(pool_step, 1)
                pool.wait_ge(pool_step, steps[0])

            def mask(g, c):
                i = HH * half_no[g] + 4 * c
                k = kind(g // 2)
                pool.wait_ge(exp_done, i + 4)
                p = pr[:, i % RING:i % RING + 4]
                if k == SELF:
                    both = p.rearrange("p h (a q) -> p h a q", q=S)[:, :, :, 0:P]
                    pool.affine_select(out=both, in_=both, compare_op=ALU.is_ge, fill=0.0, base=0,
                                       pattern=[[0, 4], [0, 2], [1, P]], channel_multiplier=-1).then_inc(masked, 1)
                else:
                    for at, m, base, s in ((0, WIN, WIN, 1), (WIN, P, 0, -1), (WW, P, 0, 1), (WW + P, WIN, 0, -1)):
                        v = p[:, :, at:at + m]
                        last = pool.affine_select(out=v, in_=v, compare_op=ALU.is_ge, fill=0.0, base=base,
                                                  pattern=[[0, 4], [s, m]], channel_multiplier=-s)
                    last.then_inc(masked, 1)

            link(pool.memset(ident[:, :], 0.0))
            pool.affine_select(out=ident[:, :], in_=ident[:, :], compare_op=ALU.not_equal, fill=1.0, base=0,
                               pattern=[[-1, P]], channel_multiplier=1).then_inc(ident_made, 1)
            link(pool.memset(identb[:, :], 0.0))
            pool.affine_select(out=identb[:, :], in_=identb[:, :], compare_op=ALU.not_equal, fill=1.0, base=0,
                               pattern=[[-1, P]], channel_multiplier=1).then_inc(ident_made, 1)
            link(pool.memset(neg_half[:, :], -0.5))

            def reciprocal_deviation(i):
                pool.wait_ge(stats_ready, i + 1)
                if i > 0:
                    pool.wait_ge(xn_ready, i)
                pool.tensor_tensor(rs[:, :], ve[:, :], neg_half[:, 0:NT], ALU.pow).then_inc(rstd_ready, 1)

            def clear_stack(buf):
                link(pool.memset(stk[:, buf].rearrange("p h s q -> p (h s q)").bitcast(F32), 0.0))
                if buf == 0:
                    reciprocal_deviation(0)
                    pool.wait_ge(rstd_ready, 1)
                pool.memset(stk[MROW:P, buf, :, 1, :].bitcast(F32), ONE_PAIR).then_inc(stacks_zero, 1)
                pool.wait_ge(stacks_zero, buf + 1)

            clear_stack(0)
            link(pool.memset(mask_c[:, :, :], 0.0))
            link(pool.memset(mask_w[:, :, :], 0.0))
            pool.affine_select(out=mask_c[:, :, :], in_=mask_c[:, :, :], compare_op=ALU.is_ge, fill=MASKED, base=0,
                               pattern=[[0, 4], [-1, P]], channel_multiplier=1).then_inc(consts_made, 1)
            for t, b1, b2 in ((0, WIN, WIN), (1, 2 * WIN, 0)):
                v = mask_w[:, t, :]
                link(pool.affine_select(out=v, in_=v, compare_op=ALU.is_ge, fill=MASKED, base=b1,
                                        pattern=[[-1, WW]], channel_multiplier=1))
                last = pool.affine_select(out=v, in_=v, compare_op=ALU.is_ge, fill=MASKED, base=b2,
                                          pattern=[[1, WW]], channel_multiplier=-1)
            last.then_inc(consts_made, 1)
            clear_stack(1)

            for g in SLOTS:
                n, h = g // 2, g % 2
                if g == -2:
                    link(pool.memset(vv[:, :, :, :, :], 0.0))
                    pool.memset(vv[:, :, :, :, HD:HD + 1], 1.0).then_inc(vv_zero, 1)
                    pool.memset(qx[:, :, :, :], 0.0).then_inc(qx_made, 1)
                    link(pool.memset(qx_cls[:, :, :, :, :], 0.0))
                    pool.memset(qx_cls[:, 0, :, :, 0:REG], 1.0).then_inc(qx_made, 1)
                    pool.wait_ge(qx_made, 2)
                for p in range(8):
                    if p in (3, 7) and g in half_no and kind(g // 2) != CLASS:
                        mask(g, p // 4)
                    for what, u in norm_tasks(g, p):
                        i = norm_order[u]
                        if what == "stats":
                            if i > 0:
                                reciprocal_deviation(i)
                        elif u >= NU or kind(u) == CROSS:
                            three = u >= NU
                            b = UNITS[u - NU][1] if three else UNITS[u][1]
                            pool.wait_ge(xn_ready, i + 1)
                            pool.wait_ge(small_in, 16 * 8)
                            for t in range(NT):
                                v = xr[:, b, t, :]
                                last = pool.tensor_tensor(v, v, o_bias[:, 1 if three else 0, :], ALU.add)
                            last.then_inc(bias_added, 1)
                    if p == 7 and g + 2 in half_no and kind((g + 2) // 2) in SPLIT_ON_POOL:
                        split_max(pool, link, g + 2)
                    if p == 0 and g + 2 in half_no and kind((g + 2) // 2) == CLASS:
                        gg = g + 2
                        buf, h0 = (gg // 2) % 2, HH * (gg % 2)
                        pool.wait_ge(stack_sem(gg), stack_count(gg))
                        if gg - 4 in half_no and kind((gg - 4) // 2) == CLASS:
                            pool.wait_ge(filled, turn("reg_scores", gg - 4) + 1)
                        pool.tensor_copy(qx[0:CLS, buf, h0:h0 + HH, 0:REG],
                                         stk[0:CLS, buf, h0:h0 + HH, 0, 0:REG]).then_inc(qx_ready, 1)
                if g == 3:
                    pool.wait_ge(w_in, 16 * 6)
                    pool.wait_ge(small_in, 16 * 8)
                    for dst, src in ((w_dh[:, 1], w[:, 1, 0:2]), (w_dh[:, 2], w[:, 2, 0:2]), (row_dh, qk_row)):
                        pool.tensor_copy(dst[:].rearrange("p a (d h) -> p a h d", d=HD),
                                         src[:].rearrange("p a (h d) -> p a h d", d=HD)).then_inc(dh_ready, 1)
                if g == 3:
                    pool.wait_ge(small_in, 16 * 8)
                    link(pool.tensor_tensor(g_sq[:, :], g_row[:, :], g_row[:, :], ALU.mult))
                    v = g_sq[:, :].rearrange("p (h d) -> p h d", d=HD)
                    link(pool.tensor_tensor(v[:, :, 0:4], v[:, :, 0:4], v[:, :, 4:8], ALU.add))
                    link(pool.tensor_tensor(v[:, :, 0:2], v[:, :, 0:2], v[:, :, 2:4], ALU.add))
                    link(pool.tensor_tensor(g_n2[:, :], v[:, :, 0], v[:, :, 1], ALU.add))
                    pool.tensor_tensor(g_rn[:, :], g_n2[:, :], neg_half[:, 0:NH], ALU.pow).then_inc(g_pow, 1)
                    pool.wait_ge(g_pow, 1)
                    pool.tensor_tensor(g_hat[:, :].rearrange("p (h d) -> p h d", d=HD),
                                       g_row[:, :].rearrange("p (h d) -> p h d", d=HD),
                                       g_rn[:, :].unsqueeze(2).broadcast_to([P, NH, HD]), ALU.mult).then_inc(g_pow, 1)
                if g == 2 * (CLASS0 - 2) + 1:
                    pool.wait_ge(ends_ready, 1)
                    pool.partition_all_reduce(ends_all[:, :], ends[:, :], P, RMAX).then_inc(ends_done, 1)


_INS = ['x', 'ctx_1024', 'L0_attn_wq', 'L0_attn_aq', 'L0_attn_bq', 'L0_attn_wk', 'L0_attn_ak', 'L0_attn_bk',
        'L0_attn_wv', 'L0_attn_av', 'L0_attn_bv', 'L0_attn_wo', 'L0_attn_ao', 'L0_attn_bo', 'L0_xattn_Wq',
        'L0_xattn_bq', 'L0_xattn_Wk', 'L0_xattn_bk', 'L0_xattn_Wv', 'L0_xattn_bv', 'L0_xattn_Wo', 'L0_xattn_bo',
        'L0_ffn_g_info', 'L0_ffn_W_qkv', 'L0_ffn_W_proj', 'L0_ffn_b_proj']
_OUTS = [((8, 256, 128), 'float32')]


def kernel(**inputs):
    import numpy as _np
    import concourse.bacc as _bacc
    from concourse import mybir as _mybir
    from concourse.bass_utils import run_bass_kernel_spmd as _run

    nc = _bacc.Bacc("TRN2", target_bir_lowering=False, num_devices=1)
    arrays, args = {}, []
    for name in _INS:
        a = _np.ascontiguousarray(inputs[name])
        arrays[f"in_{name}_dram"] = a
        args.append(nc.dram_tensor(f"in_{name}_dram", a.shape, _mybir.dt.from_np(a.dtype), kind="ExternalInput").ap())
    for i, (shape, dtype) in enumerate(_OUTS):
        dt = _mybir.dt.from_np(_np.dtype(dtype))
        args.append(nc.dram_tensor(f"out_{i}_dram", shape, dt, kind="ExternalOutput").ap())
    layer_kernel(nc, *args)
    r = _run(nc, [arrays], core_ids=[0])
    got = tuple(r.results[0][f"out_{i}_dram"] for i in range(len(_OUTS)))
    return got[0]
```
